# Optimizing a Trainium2 kernel written in Bass

```python
import numpy as np
import jax
import jax.numpy as jnp

def _softmax(x, axis=-1):
    return jax.nn.softmax(x, axis=axis)

def _gelu(x):
    return jax.nn.gelu(x, approximate=True)

def _silu(x):
    return jax.nn.silu(x)

def _sigmoid(x):
    return jax.nn.sigmoid(x)

def _layernorm(x, axis=-1, eps=1e-05):
    m = jnp.mean(x, axis=axis, keepdims=True)
    v = jnp.var(x, axis=axis, keepdims=True)
    return (x - m) / jnp.sqrt(v + eps)

def _scatter_add(tgt, idx, src, axis=0):
    return tgt.at[idx].add(src)

def _segment_sum(src, seg, n):
    return jax.ops.segment_sum(src, seg, n)
kernel_name = 'mk_macaron_d1_jaxref_r8_615368'

def setup_inputs(seed: int=0):
    np.random.seed(seed)
    _w = jnp.asarray

    def _L0_attn_setup():
        import jax, jax.numpy as jnp
        import numpy as np
        EPS = 1e-05
        NUM_HEADS = 16
        FEATURE_DIM = 16
        CHUNK = 64

        def _phi(x):
            f = x.shape[-1]
            return (x[..., :, None] * x[..., None, :]).reshape(*x.shape[:-1], f * f)
        key = jax.random.key(seed)
        ks = jax.random.split(key, 5)
        b, l, d = (4, 256, 128)
        h, f = (NUM_HEADS, FEATURE_DIM)
        hd = d // h
        scale = 0.02
        return {'hidden_states': jax.random.normal(ks[0], (b, l, d), jnp.float32), 'Wq': jax.random.normal(ks[1], (d, h * f), jnp.float32) * scale, 'Wk': jax.random.normal(ks[2], (d, h * f), jnp.float32) * scale, 'Wv': jax.random.normal(ks[3], (d, h * hd), jnp.float32) * scale, 'Wo': jax.random.normal(ks[4], (h * hd, d), jnp.float32) * scale}
    _L0_attn_in = _L0_attn_setup()

    def _L0_ffn_setup():
        import jax, jax.numpy as jnp
        import numpy as np
        K = 2
        CAP_FACTOR = 1.25
        key = jax.random.key(seed)
        ks = jax.random.split(key, 6)
        B, T, C, H, E = (8, 256, 128, 512, 8)
        return {'x': jax.random.normal(ks[0], (B, T, C), dtype=jnp.float32), 'Wr': jax.random.normal(ks[1], (C, E), dtype=jnp.float32) * 0.02, 'W1': jax.random.normal(ks[2], (E, C, H), dtype=jnp.float32) * 0.02, 'b1': jax.random.normal(ks[3], (E, H), dtype=jnp.float32) * 0.02, 'W2': jax.random.normal(ks[4], (E, H, C), dtype=jnp.float32) * 0.02, 'b2': jax.random.normal(ks[5], (E, C), dtype=jnp.float32) * 0.02}
    _L0_ffn_in = _L0_ffn_setup()
    _d = {'L0_attn_hidden_states': _L0_attn_in['hidden_states'], 'L0_attn_Wq': _L0_attn_in['Wq'], 'L0_attn_Wk': _L0_attn_in['Wk'], 'L0_attn_Wv': _L0_attn_in['Wv'], 'L0_attn_Wo': _L0_attn_in['Wo'], 'L0_ffn_Wr': _L0_ffn_in['Wr'], 'L0_ffn_W1': _L0_ffn_in['W1'], 'L0_ffn_b1': _L0_ffn_in['b1'], 'L0_ffn_W2': _L0_ffn_in['W2'], 'L0_ffn_b2': _L0_ffn_in['b2']}
    _x0 = _d['L0_attn_hidden_states']
    _d['L0_attn_hidden_states'] = jax.random.normal(jax.random.fold_in(jax.random.key(seed), 1), (8, 256, 128), dtype=_x0.dtype)
    del _x0
    return _d

def reference(L0_attn_hidden_states, L0_attn_Wq, L0_attn_Wk, L0_attn_Wv, L0_attn_Wo, L0_ffn_Wr, L0_ffn_W1, L0_ffn_b1, L0_ffn_W2, L0_ffn_b2):

    def _L0_attn_ref(hidden_states, Wq, Wk, Wv, Wo):
        import jax, jax.numpy as jnp
        import numpy as np
        EPS = 1e-05
        NUM_HEADS = 16
        FEATURE_DIM = 16
        CHUNK = 64

        def _phi(x):
            f = x.shape[-1]
            return (x[..., :, None] * x[..., None, :]).reshape(*x.shape[:-1], f * f)
        b, l, d = hidden_states.shape
        h, f = (NUM_HEADS, FEATURE_DIM)
        hd = d // h
        q = (hidden_states @ Wq).reshape(b, l, h, f).transpose(0, 2, 1, 3)
        k = (hidden_states @ Wk).reshape(b, l, h, f).transpose(0, 2, 1, 3)
        v = (hidden_states @ Wv).reshape(b, l, h, hd).transpose(0, 2, 1, 3)
        q = q * f ** (-0.5)
        n = l // CHUNK
        qc = q.reshape(b, h, n, CHUNK, f)
        kc = k.reshape(b, h, n, CHUNK, f)
        vc = v.reshape(b, h, n, CHUNK, hd)
        phi_q = _phi(qc)
        phi_k = _phi(kc)
        mask = jnp.tril(jnp.ones((CHUNK, CHUNK), dtype=q.dtype))

        def step(carry, inp):
            S, z = carry
            pq, pk, qi, ki, vi = inp
            inter_o = jnp.einsum('bhcf,bhfd->bhcd', pq, S)
            inter_z = jnp.einsum('bhcf,bhf->bhc', pq, z)
            A = jnp.einsum('bhcf,bhsf->bhcs', qi, ki) ** 2 * mask
            intra_o = jnp.einsum('bhcs,bhsd->bhcd', A, vi)
            intra_z = A.sum(-1)
            o = (inter_o + intra_o) / (inter_z + intra_z + EPS)[..., None]
            S = S + jnp.einsum('bhcf,bhcd->bhfd', pk, vi)
            z = z + pk.sum(2)
            return ((S, z), o)
        f2 = f * f
        S0 = jnp.zeros((b, h, f2, hd), q.dtype)
        z0 = jnp.zeros((b, h, f2), q.dtype)
        xs = (jnp.moveaxis(phi_q, 2, 0), jnp.moveaxis(phi_k, 2, 0), jnp.moveaxis(qc, 2, 0), jnp.moveaxis(kc, 2, 0), jnp.moveaxis(vc, 2, 0))
        _, o = jax.lax.scan(step, (S0, z0), xs)
        o = jnp.moveaxis(o, 0, 2).reshape(b, h, l, hd)
        o = o.transpose(0, 2, 1, 3).reshape(b, l, h * hd)
        return o @ Wo

    def _L0_ffn_ref(x, Wr, W1, b1, W2, b2):
        import jax, jax.numpy as jnp
        import numpy as np
        K = 2
        CAP_FACTOR = 1.25
        B, T, C = x.shape
        E = Wr.shape[1]
        capacity = int(T / E * CAP_FACTOR)
        probs = jax.nn.softmax(x @ Wr, axis=-1)
        topk_probs, topk_experts = jax.lax.top_k(probs, K)
        S = T * K
        e_flat = topk_experts.reshape(B, S)
        p_flat = topk_probs.reshape(B, S)
        x_rep = jnp.repeat(x, K, axis=1)
        onehot = jax.nn.one_hot(e_flat, E, dtype=jnp.int32)
        pos_all = jnp.cumsum(onehot, axis=1) - onehot
        pos = jnp.take_along_axis(pos_all, e_flat[..., None], axis=-1)[..., 0]
        keep = pos < capacity
        pos_c = jnp.minimum(pos, capacity - 1)
        b_idx = jnp.broadcast_to(jnp.arange(B)[:, None], (B, S))
        buf = jnp.zeros((E, B, capacity, C), dtype=x.dtype)
        buf = buf.at[e_flat, b_idx, pos_c].add(x_rep * keep[..., None].astype(x.dtype))
        h = jax.nn.relu(jnp.einsum('ebnc,ech->ebnh', buf, W1) + b1[:, None, None, :])
        y = jnp.einsum('ebnh,ehc->ebnc', h, W2) + b2[:, None, None, :]
        y_tok = y[e_flat, b_idx, pos_c]
        y_tok = y_tok * keep[..., None].astype(x.dtype) * p_flat[..., None]
        out = y_tok.reshape(B, T, K, C).sum(axis=2)
        return out
    x = L0_attn_hidden_states
    x = x + 0.5 * _L0_ffn_ref(_layernorm(x, axis=-1), L0_ffn_Wr, L0_ffn_W1, L0_ffn_b1, L0_ffn_W2, L0_ffn_b2)
    x = x + _L0_attn_ref(_layernorm(x, axis=-1), L0_attn_Wq, L0_attn_Wk, L0_attn_Wv, L0_attn_Wo)
    x = x + 0.5 * _L0_ffn_ref(_layernorm(x, axis=-1), L0_ffn_Wr, L0_ffn_W1, L0_ffn_b1, L0_ffn_W2, L0_ffn_b2)
    return x

_drawn_inputs = setup_inputs


def setup_inputs(seed=0):
    import zlib

    import numpy as np

    out = dict(_drawn_inputs(seed))
    spreads = {}
    factors = {'L0_attn_Wq': 6.404,
     'L0_attn_Wk': 6.228,
     'L0_attn_Wv': 4.762,
     'L0_attn_Wo': 4.704,
     'L0_ffn_Wr': 4.659,
     'L0_ffn_W1': 5.232,
     'L0_ffn_b1': 8.0,
     'L0_ffn_W2': 4.298,
     'L0_ffn_b2': 8.0}
    for name, (base, spread) in spreads.items():
        noise = np.random.default_rng([zlib.crc32(name.encode()), seed]).standard_normal(out[name].shape)
        drawn = base * np.exp(spread * noise) if base else spread * noise
        out[name] = jnp.asarray(drawn.astype(out[name].dtype))
    for name, factor in factors.items():
        out[name] = (out[name] * factor).astype(out[name].dtype)
    return out
```

```python
import concourse.bass as bass
from concourse import mybir
from contextlib import ExitStack

P = 128
B, T, C = 8, 256, 128
E, HID, K_TOP = 8, 512, 2
CAP = int(T / E * 1.25)
HEADS, F, HD = 16, 16, C // 16
TT = T // P
NT = B * TT
GB = 4
NG = B // GB
GT = GB * TT
SLOTS = E * CAP
KT = 3
SP_ = KT * P
GS = GB * CAP
HC = HID // P
NP = B // 2
PT = 2 * T
VW = 32
LN_EPS = 1e-5
DEN_EPS = 1e-5
BIG = 1e30
HEAD_ORDER = [0, 2, 4, 6, 1, 3, 5, 7, 8, 10, 12, 14, 9, 11, 13, 15]
A_RING = 6
MISC = ("bt", "xt", "lg", "ps", "ot", "pw", "dph", "dpl", "yt", "cb", "qk", "v", "ox", "oT", "wo")


def experts(l, g, hooks):
    out = [("up", l, g, 0)]
    for e in range(E):
        if e + 1 < E:
            out.append(("up", l, g, e + 1))
        out.append(("down", l, g, e))
        out += hooks.get(e, [])
    return out


def stage_order():
    def norm(*key):
        return [("ln1",) + key, ("ln2",) + key]

    def logits(l, g):
        return [("xt", "f", l, g, 0), ("xt", "f", l, g, 1), ("lg", l, g)]

    def spread(l, g):
        return [("ot", l, g, i) for i in range(GB)] + [("pw", l, g)]

    def dispatch(l, g):
        return [(kind, l, g, i) for i in range(GB) for kind in ("dph", "dpl")]

    def turn_y(l, g):
        return [("yt", l, g, i) for i in range(GB)]

    def combine(l, g):
        return [("cb", l, g, i) for i in range(GB // 2)]

    def project(p):
        return ([("xt", "a", p, 0)] + [("qk", p, w, c) for w in range(2) for c in range(2)] + [("v", 2 * p)])

    order = [("bt",)]
    order += norm("f", 0, 0) + [("ln1", "f", 0, 1)] + logits(0, 0) + [("ln2", "f", 0, 1), ("ps", 0, 0)]
    order += spread(0, 0) + dispatch(0, 0)
    order += experts(0, 0, {0: logits(0, 1), 3: [("ps", 0, 1)], 5: spread(0, 1), 6: dispatch(0, 1)})
    order += experts(0, 1, {0: turn_y(0, 0), 1: combine(0, 0), 2: norm("a", 0), 3: project(0) + [("v", 1), ("ld", 0), ("ld", 1)],
                            4: norm("a", 1), 6: project(1) + [("v", 3)]})
    order += turn_y(0, 1)
    hooks = {(0, 1): combine(0, 1), (0, 3): norm("a", 2), (1, 1): project(2) + [("ld", 2)], (1, 7): [("ld", 3)],
             (2, 0): norm("a", 3), (2, 1): [("v", 5)], (4, 1): [("v", 7)],
             (2, 7): [("ld", 4)], (3, 1): project(3), (3, 7): [("ld", 5)],
             (4, 7): [("ld", 6)], (5, 7): [("ld", 7)],
             (5, 1): norm("f", 1, 0), (5, 5): logits(1, 0), (6, 1): [("ps", 1, 0)], (6, 5): spread(1, 0),
             (7, 1): dispatch(1, 0)}
    pairs = [(b, m) for b in range(B) for m in range(HEADS // 2)]

    def values(quad):
        b, q = divmod(quad, HEADS // 4)
        return [("av", b, q)] + ([("xe", b, q // 2)] if q % 2 else [])

    for n, (b, m) in enumerate(pairs):
        order.append(("sc", b, m))
        if n >= 3 and n % 2:
            order += values((n - 3) // 2)
        if b and m in (3, 5, 7):
            order.append(({3: "ox", 5: "oT", 7: "wo"}[m], b - 1))
        order += hooks.get((b, m), [])
    order += values(B * HEADS // 4 - 1)
    order += experts(1, 0, {0: [("ox", B - 1), ("oT", B - 1)], 1: [("wo", B - 1)] + norm("f", 1, 1),
                            3: logits(1, 1), 4: [("ps", 1, 1)], 5: spread(1, 1), 6: dispatch(1, 1)})
    order += experts(1, 1, {0: turn_y(1, 0), 1: combine(1, 0)})
    order += turn_y(1, 1) + combine(1, 1)
    return order


def macaron_program(nc, x_in, wq_in, wk_in, wv_in, wo_in, wr_in, w1_in, b1_in, w2_in, b2_in, out):
    f32, f16, i32 = mybir.dt.float32, mybir.dt.float16, mybir.dt.int32
    ALU, ACT, AX = mybir.AluOpType, mybir.ActivationFunctionType, mybir.AxisListType

    ORDER = stage_order()
    nth, seen, count_of = {}, {}, {}
    item = {}
    for s in ORDER:
        nth[s] = seen.get(s[0], 0)
        count_of[s] = dict(seen)
        seen[s[0]] = nth[s] + 1
        if s[0] in MISC:
            item[s] = len(item)

    def before(stage, kind):
        return count_of[stage].get(kind, 0)

    ctx = ExitStack()
    with ctx:
        def sb(name, shape, dt=f32):
            return ctx.enter_context(nc.sbuf_tensor(name, shape, dt))

        def sem(name):
            return ctx.enter_context(nc.semaphore(name))

        x = sb("x", [P, NT, C])
        stats = sb("stats", [P, 2, GT, 6])
        meanvar = sb("meanvar", [P, 2, GT, 2])
        std = sb("std", [P, 2, GT])
        rstd = sb("rstd", [P, 2, GT])
        xn = sb("xn", [P, GT, C])
        xf = sb("xf", [P, 2, 2, GT, C], f16)
        xa = sb("xa", [P, 2, 4, C], f16)
        xTf = sb("xTf", [P, 2, GT, P], f16)
        xTa = sb("xTa", [P, 2, 4, P], f16)
        lg = sb("lg", [P, GT, E])
        lmax = sb("lmax", [P, GT])
        ldiff = sb("ldiff", [P, GT, E])
        lexp = sb("lexp", [P, GT, E])
        cand = sb("cand", [P, GT, E])
        cmax = sb("cmax", [P, GT])
        sel1 = sb("sel1", [P, GT, E])
        rest = sb("rest", [P, GT, E])
        esum = sb("esum", [P, GT])
        prob = sb("prob", [P, GT, E])
        p16 = sb("p16", [P, GT, 2, E], f16)
        sel = sb("sel", [P, TT, GB, E], f16)
        key = sb("key", [P, TT, GB, E])
        oh = sb("oh", [P, GT, SP_], f16)
        ohT = sb("ohT", [P, 2, GB, KT, T], f16)
        pmask = sb("pmask", [P, GB * KT * 2 * E])
        pslot = sb("pslot", [P, 2, GB * KT])
        xe = sb("xe", [P, 2, 2, E, GS], f16)
        hid = sb("hid", [P, 2, HC, GS])
        yT = sb("yT", [P, 2, GB, SP_])
        yp = sb("yp", [P, 2, SP_])
        y16 = sb("y16", [P, 2, GB, SP_], f16)
        w1 = sb("w1", [P, 2, E, HID], f16)
        w2 = sb("w2", [P, E, HC, C])
        bias_rows = sb("bias_rows", [E * HC + E, P])
        biasT = sb("biasT", [P, E * HC + E])
        wsm = sb("wsm", [P, 2, 8 + 3 * 256 - 128], f16)
        wo = sb("wo", [P, C])
        qk16 = sb("qk16", [P, 2, 2, 2, PT], f16)
        stack = sb("stack", [P, 2, 2, HEADS, T], f16)
        amat = sb("amat", [P, A_RING, 2, T + P])
        wsml = amat[:, 0, :, :].rearrange("p h c -> p (h c)")[:, 0:648]
        w1s = amat[:, 1:3, :, :].rearrange("p s h c -> p s (h c)")[:, :, 0:HID]
        vst = sb("vst", [P, 4, TT, HEADS // 2, 2 * VW])
        xy = sb("xy", [P, 2, 2, T])
        den = sb("den", [P, 16, 2])
        rden = sb("rden", [P, 16, 2])
        onorm = sb("onorm", [P, TT, C])
        oT = sb("oT", [P, T])
        eps = sb("eps", [P, 1])
        ident = sb("ident", [P, P])
        ident16 = sb("ident16", [P, P], f16)
        ones16 = sb("ones16", [P, P], f16)
        upper16 = sb("upper16", [P, P], f16)
        iota_i = sb("iota_i", [P, CAP], i32)
        iota = sb("iota", [P, CAP], f16)
        rank_i = sb("rank_i", [P, GT, E], i32)
        rank = sb("rank", [P, GT, E])

        psS = ctx.enter_context(nc.psum_tensor("psS", [P, 4, 512], f32))
        psY = ctx.enter_context(nc.psum_tensor("psY", [P, 2, 512], f32))
        psM = ctx.enter_context(nc.psum_tensor("psM", [P, 2, 512], f32))

        scr = nc.dram_tensor("qk_parts", [NP, 2, 2, HEADS * F, PT], f16, kind="Internal").ap()

        x_loaded = [sem(f"x_loaded{c}") for c in range(4)]
        wr_loaded, wqkv_loaded = sem("wr_loaded"), sem("wqkv_loaded")
        bias_loaded = sem("bias_loaded")
        w1_loaded = [sem(f"w1_loaded{c}") for c in range(2)]
        w2_loaded = [sem(f"w2_loaded{c}") for c in range(E)]
        wo_loaded = sem("wo_loaded")
        consts_made = sem("consts_made")
        zeros_made = sem("zeros_made")
        wsm_hi, wsm_split = sem("wsm_hi"), sem("wsm_split")
        w1_hi, w1_split = sem("w1_hi"), sem("w1_split")
        bank_ready = [sem(f"bank_ready{c}") for c in range(2)]
        bank_taken = [sem(f"bank_taken{c}") for c in range(2)]
        var_ready, std_ready, x_split = sem("var_ready"), sem("std_ready"), sem("x_split")
        diff_ready, exp_ready = sem("diff_ready"), sem("exp_ready")
        sel_ready, prob_split, oh_ready = sem("sel_ready"), sem("prob_split"), sem("oh_ready")
        h_ready, h_act, h_dve = sem("h_ready"), sem("h_act"), sem("h_dve")
        y_ready, y_taken = sem("y_ready"), sem("y_taken")
        yh_ready, yl_ready = sem("yh_ready"), sem("yl_ready")
        qk_hi = sem("qk_hi")
        qk_stored = [sem(f"qk_stored{c}") for c in range(4)]
        stack_loaded = [sem(f"stack_loaded{c}") for c in range(2)]
        s_ready, s_taken, a_ready = sem("s_ready"), sem("s_taken"), sem("a_ready")
        av_done, xy_taken = sem("av_done"), sem("xy_taken")
        dve_step, pool_step = sem("dve_step"), sem("pool_step")
        stored = sem("stored")

        def wait_ready(eng, stage):
            k = item[stage]
            eng.wait_ge(bank_ready[k % 2], k // 2 + 1)

        def wait_taken(eng, stage):
            k = item[stage]
            eng.wait_ge(bank_taken[k % 2], k // 2 + 1)

        def bank(stage):
            return psM[:, item[stage] % 2, :]

        def bank16(stage):
            return bank(stage).bitcast(f16)

        def taken(stage):
            return bank_taken[item[stage] % 2]

        def tiles_of(key_):
            if key_[0] == "f":
                return list(range(key_[2] * GT, (key_[2] + 1) * GT))
            return list(range(4 * key_[1], 4 * key_[1] + 4))

        def parity(l, g):
            return (l * NG + g) % 2

        WR, WQ, WV = slice(0, 8), (8, 264), 520

        block = ctx.enter_context(nc.Block())

        @block.sync
        def _(sp):
            for c in range(4):
                sp.dma_start(x[:, 4 * c:4 * c + 4, :],
                             x_in[2 * c:2 * c + 2].rearrange("b (t p) c -> p (b t) c", p=P)).then_inc(x_loaded[c], 16)
                if c == 0:
                    sp.dma_start(wsml[:, WR], wr_in).then_inc(wr_loaded, 16)
                    sp.dma_start(bias_rows[0:E * HC, :], b1_in.rearrange("e (h c) -> (e h) c", c=P)).then_inc(bias_loaded, 16)
                    sp.dma_start(bias_rows[E * HC:, :], b2_in).then_inc(bias_loaded, 16)
            sp.dma_start(wsml[:, 8:264], wq_in).then_inc(wqkv_loaded, 16)
            sp.dma_start(wsml[:, 264:520], wk_in).then_inc(wqkv_loaded, 16)
            sp.dma_start(wsml[:, 520:648], wv_in).then_inc(wqkv_loaded, 16)
            sp.dma_start(wo[:, :], wo_in).then_inc(wo_loaded, 16)
            for e in range(E):
                if e >= 2:
                    sp.wait_ge(w1_split, e - 1)
                sp.dma_start(w1s[:, e % 2, :], w1_in[e]).then_inc(w1_loaded[e % 2], 16)
                sp.dma_start(w2[:, e, :, :], w2_in[e].rearrange("(h p) c -> p h c", p=P)).then_inc(w2_loaded[e], 16)
            n_stored = 0
            for s in ORDER:
                if s[0] == "qk":
                    _, p, w, c = s
                    wait_taken(sp, s)
                    sp.dma_start(scr[p, w, :, c * P:(c + 1) * P, :].rearrange("a r t -> r a t"),
                                 qk16[:, w, c, :, :]).then_inc(qk_stored[2 * w + c], 16)
                elif s[0] == "ld":
                    b = s[1]
                    p = b // 2
                    for c in range(4):
                        sp.wait_ge(qk_stored[c], 16 * (p + 1))
                    if b >= 2:
                        sp.wait_ge(s_ready, (b - 1) * HEADS // 2)
                    for w in range(2):
                        for r in range(4):
                            part = (r % 2) if w == 0 else (r // 2)
                            src = scr[p, w, part, :, (b % 2) * T:(b % 2 + 1) * T].rearrange("(h f) t -> f h t", f=F)
                            sp.dma_start(stack[r * F:(r + 1) * F, b % 2, w, :, :], src).then_inc(stack_loaded[b % 2], 16)
                elif s[0] == "cb" and s[1] == 1:
                    _, _, g, i = s
                    wait_taken(sp, s)
                    b0 = g * GB + 2 * i
                    sp.dma_start(out[b0:b0 + 2].rearrange("b (t p) c -> p (b t) c", p=P),
                                 x[:, TT * b0:TT * b0 + 4, :]).then_inc(stored, 16)
                    n_stored += 1
            sp.wait_ge(stored, 16 * n_stored)

        @block.gpsimd
        def _(pool):
            steps = [0]

            def link(ins):
                steps[0] += 1
                ins.then_inc(pool_step, 1)
                pool.wait_ge(pool_step, steps[0])

            pool.memset(eps[:, :], LN_EPS)
            pool.memset(ident16[:, :], 0.0)
            pool.memset(ones16[:, :], 1.0)
            pool.iota(iota_i[:, :], pattern=[[1, CAP]], base=1, channel_multiplier=0)
            pool.iota(rank_i[:, :, :], pattern=[[0, GT], [-1, E]], base=E, channel_multiplier=0)
            link(pool.memset(ident[:, :], 0.0))
            pool.affine_select(out=ident16[:, :], in_=ident16[:, :], pattern=[[-1, P]], compare_op=ALU.not_equal,
                               fill=1.0, base=0, channel_multiplier=1)
            pool.affine_select(out=ident[:, :], in_=ident[:, :], pattern=[[-1, P]], compare_op=ALU.not_equal,
                               fill=1.0, base=0, channel_multiplier=1)
            pool.affine_select(out=upper16[:, :], in_=ones16[:, :], pattern=[[1, P]], compare_op=ALU.is_gt,
                               fill=0.0, base=0, channel_multiplier=-1)
            pool.tensor_copy(iota[:, :], iota_i[:, :])
            pool.tensor_copy(rank[:, :, :], rank_i[:, :, :]).then_inc(consts_made, 1)
            pool.memset(oh[:, :, SLOTS:], 0.0)
            pm = pmask[:, :].rearrange("p (b k a e) -> p b k a e", b=GB, k=KT, a=2)
            link(pool.memset(pmask[:, :], 1.0))
            link(pool.affine_select(out=pm, in_=pm, pattern=[[0, GB], [P, KT], [0, 2], [-CAP, E]],
                                    compare_op=ALU.is_ge, fill=0.0, base=0, channel_multiplier=1))
            last = pool.affine_select(out=pm, in_=pm, pattern=[[0, GB], [-P, KT], [0, 2], [CAP, E]],
                                      compare_op=ALU.is_gt, fill=0.0, base=CAP, channel_multiplier=-1)
            last.then_inc(consts_made, 1)

            def split_small(n, cols):
                pool.wait_ge(wsm_hi, n)
                pool.tensor_tensor(wsm[:, 1, cols], wsml[:, cols], wsm[:, 0, cols], ALU.subtract).then_inc(wsm_split, 1)

            split_small(1, WR)
            for e in range(E):
                pool.wait_ge(w1_hi, e + 1)
                pool.tensor_tensor(w1[:, 1, e, :], w1s[:, e % 2, :], w1[:, 0, e, :], ALU.subtract).then_inc(w1_split, 1)
            pool.memset(yT[:, :, :, SLOTS:], 0.0).then_inc(zeros_made, 1)
            split_small(2, slice(8, 648))
            pool.wait_ge(wsm_split, 2)
            link(pool.memset(stack[4 * F:, :, :, :, :], 0.0))
            link(pool.memset(vst[:, :, :, :, :], 0.0))
            pool.memset(vst[:, :, :, :, 2 * HD:2 * HD + 1], 1.0)
            pool.memset(vst[:, :, :, :, VW + 2 * HD + 1:VW + 2 * HD + 2], 1.0).then_inc(zeros_made, 1)
            for s in ORDER:
                if s[0] == "yt":
                    i = s[3]
                    n = nth[s]
                    pool.wait_ge(yh_ready, n + 1)
                    pool.tensor_tensor(y16[:, 1, i, :], yp[:, n % 2, :], y16[:, 0, i, :], ALU.subtract).then_inc(yl_ready, 1)
                elif s[0] == "sc":
                    n = nth[s]
                    pool.wait_ge(s_taken, n + 1)
                    d = amat[:, n % A_RING, :, 0:2 * P].rearrange("p h (c t) -> p h c t", t=P)
                    pool.affine_select(out=d, in_=d, pattern=[[0, 2], [0, 2], [1, P]], compare_op=ALU.is_ge,
                                       fill=0.0, base=0, channel_multiplier=-1).then_inc(a_ready, 1)

        @block.scalar
        def _(act):
            act.wait_ge(wr_loaded, 16)
            act.activation(wsm[:, 0, WR], wsml[:, WR], ACT.Copy).then_inc(wsm_hi, 1)

            def split_w1(e):
                act.wait_ge(w1_loaded[e % 2], 16 * (e // 2 + 1))
                act.activation(w1[:, 0, e, :], w1s[:, e % 2, :], ACT.Copy).then_inc(w1_hi, 1)

            n_w1 = 0
            for s in ORDER:
                kind = s[0]
                n = nth[s]
                if kind == "ln1":
                    nt = len(tiles_of(s[1:]))
                    if n == 0:
                        act.wait_ge(consts_made, 1)
                    act.wait_ge(var_ready, n + 1)
                    act.activation(std[:, n % 2, 0:nt], meanvar[:, n % 2, 0:nt, 1], ACT.Sqrt,
                                   bias=eps[:, :]).then_inc(std_ready, 1)
                elif kind == "lg":
                    act.wait_ge(diff_ready, n + 1)
                    act.activation(lexp[:, :, :], ldiff[:, :, :], ACT.Exp).then_inc(exp_ready, 1)
                elif kind == "ot":
                    _, l, g, i = s
                    wait_ready(act, s)
                    act.activation(ohT[:, parity(l, g), i, :, :].rearrange("p k t -> p (k t)"),
                                   bank16(s)[:, 0:KT * T], ACT.Copy).then_inc(taken(s), 1)
                elif kind == "dph":
                    _, l, g, i = s
                    wait_ready(act, s)
                    act.activation(xe[:, parity(l, g), 0, :, i * CAP:(i + 1) * CAP],
                                   bank(s)[:, 0:SLOTS].rearrange("p (e c) -> p e c", e=E), ACT.Copy).then_inc(taken(s), 1)
                elif kind == "up":
                    _, l, g, e = s
                    if n >= 2:
                        act.wait_ge(y_ready, n - 1)
                    act.wait_ge(h_ready, 2 * n + 1)
                    for c in range(2):
                        ins = act.activation(hid[:, n % 2, c, :], psS[:, 2 * (n % 2), c * GS:(c + 1) * GS], ACT.Relu,
                                             bias=biasT[:, e * HC + c:e * HC + c + 1])
                    ins.then_inc(h_act, 1)
                elif kind == "down":
                    _, l, g, e = s
                    if n == 0:
                        act.wait_ge(zeros_made, 1)
                    act.wait_ge(y_ready, n + 1)
                    act.activation(yT[:, parity(l, g), :, e * CAP:(e + 1) * CAP],
                                   psY[:, n % 2, 0:GS].rearrange("p (b c) -> p b c", b=GB), ACT.Identity,
                                   bias=biasT[:, E * HC + e:E * HC + e + 1]).then_inc(y_taken, 1)
                elif kind == "yt":
                    i = s[3]
                    wait_taken(act, s)
                    act.activation(y16[:, 0, i, :], yp[:, n % 2, :], ACT.Copy).then_inc(yh_ready, 1)
                elif kind == "qk":
                    _, p, w, c = s
                    wait_ready(act, s)
                    if p:
                        act.wait_ge(qk_stored[2 * w + c], 16 * p)
                    act.activation(qk16[:, w, c, 0, :], bank(s), ACT.Copy, scale=F ** -0.5 if w == 0 else 1.0)\
                        .then_inc(qk_hi, 1)
                elif kind == "sc":
                    act.wait_ge(s_ready, n + 1)
                    if n >= A_RING:
                        act.wait_ge(av_done, (n - A_RING) // 2 + 1)
                    act.activation(amat[:, n % A_RING, :, :], psS[:, 2 * (n % 2):2 * (n % 2) + 2, 0:T + P], ACT.Square)\
                        .then_inc(s_taken, 1)
                elif kind == "oT":
                    wait_ready(act, s)
                    act.activation(oT[:, :], bank(s)[:, 0:T], ACT.Copy).then_inc(taken(s), 1)
                if s == ("lg", 0, 0):
                    while n_w1 < 3:
                        split_w1(n_w1)
                        n_w1 += 1
                elif kind == "ot" and s[1:3] == (0, 0):
                    split_w1(n_w1)
                    n_w1 += 1
                elif s == ("dph", 0, 0, 1):
                    split_w1(n_w1)
                    n_w1 += 1
                    act.wait_ge(wqkv_loaded, 48)
                    act.activation(wsm[:, 0, 8:648], wsml[:, 8:648], ACT.Copy).then_inc(wsm_hi, 1)
            assert n_w1 == E

        @block.vector
        def _(dve):
            steps = [0]

            def link(ins):
                steps[0] += 1
                ins.then_inc(dve_step, 1)
                dve.wait_ge(dve_step, steps[0])

            def over_experts(t):
                return t[:, :].unsqueeze(2).broadcast_to([P, GT, E])

            dve.wait_ge(consts_made, 1)
            for s in ORDER:
                kind = s[0]
                n = nth[s]
                if kind == "bt":
                    wait_ready(dve, s)
                    dve.tensor_copy(biasT[:, :], bank(s)[:, 0:E * HC + E]).then_inc(taken(s), 1)
                elif kind == "ln1":
                    tiles = tiles_of(s[1:])
                    if s[1] == "a":
                        p = s[1 + 1]
                        wait_taken(dve, ("cb", 0, p // 2, p % 2))
                    elif s[2] == 1:
                        wait_taken(dve, ("wo", tiles[-1] // TT))
                    for i, t in enumerate(tiles):
                        if s[1:3] == ("f", 0) and t % 4 == 0:
                            dve.wait_ge(x_loaded[t // 4], 16)
                        ins = dve.bn_stats(stats[:, n % 2, i, :], x[:, t, :])
                    link(ins)
                    for i, t in enumerate(tiles):
                        ins = dve.bn_aggr(meanvar[:, n % 2, i, :], stats[:, n % 2, i, :])
                    ins.then_inc(var_ready, 1)
                elif kind == "ln2":
                    tiles = tiles_of(s[1:])
                    nt = len(tiles)
                    dve.wait_ge(std_ready, n + 1)
                    link(dve.reciprocal(rstd[:, n % 2, 0:nt], std[:, n % 2, 0:nt]))
                    for i, t in enumerate(tiles):
                        ins = dve.tensor_scalar(xn[:, i, :], x[:, t, :], meanvar[:, n % 2, i, 0:1],
                                                rstd[:, n % 2, i:i + 1], ALU.subtract, ALU.mult)
                    link(ins)
                    parts = xf[:, parity(*s[2:])] if s[1] == "f" else xa[:, :, :, :]
                    if s[1] == "a" and s[2]:
                        wait_ready(dve, ("xt", "a", s[2] - 1, 0))
                    elif s[1] == "f" and s[2]:
                        wait_ready(dve, ("dpl", 0, s[3], GB - 1))
                    link(dve.tensor_copy(parts[:, 0, :, :], xn[:, 0:nt, :]))
                    dve.tensor_tensor(parts[:, 1, :, :], xn[:, 0:nt, :], parts[:, 0, :, :], ALU.subtract)\
                        .then_inc(x_split, 1)
                elif kind == "xt":
                    q = s[-1]
                    dst = xTf[:, :, 4 * q:4 * q + 4, :] if s[1] == "f" else xTa[:, :, :, :]
                    wait_ready(dve, s)
                    dve.tensor_copy(dst.rearrange("p a t c -> p a (t c)"),
                                    bank16(s).rearrange("p (a n) -> p a n", a=2)).then_inc(taken(s), 1)
                elif kind == "lg":
                    wait_ready(dve, s)
                    ins = dve.tensor_reduce(lg[:, :, :], bank(s)[:, 0:GT * 2 * E]
                                            .rearrange("p (t a e) -> p t e a", t=GT, a=2), AX.X, ALU.add)
                    ins.then_inc(taken(s), 1)
                    wait_taken(dve, s)
                    link(dve.tensor_reduce(lmax[:, :], lg[:, :, :], AX.X, ALU.max))
                    dve.tensor_tensor(ldiff[:, :, :], lg[:, :, :], over_experts(lmax), ALU.subtract).then_inc(diff_ready, 1)
                    dve.wait_ge(diff_ready, n + 1)
                    link(dve.scalar_tensor_tensor(out=cand[:, :, :], in0=ldiff[:, :, :], scalar=0.0, in1=rank[:, :, :],
                                                  op0=ALU.is_ge, op1=ALU.mult))
                    link(dve.tensor_reduce(cmax[:, :], cand[:, :, :], AX.X, ALU.max))
                    link(dve.tensor_tensor(sel1[:, :, :], cand[:, :, :], over_experts(cmax), ALU.is_equal))
                    link(dve.scalar_tensor_tensor(out=rest[:, :, :], in0=sel1[:, :, :], scalar=-BIG, in1=ldiff[:, :, :],
                                                  op0=ALU.mult, op1=ALU.add))
                    link(dve.tensor_reduce(lmax[:, :], rest[:, :, :], AX.X, ALU.max))
                    link(dve.tensor_tensor(cand[:, :, :], rest[:, :, :], over_experts(lmax), ALU.is_ge))
                    link(dve.tensor_tensor(cand[:, :, :], cand[:, :, :], rank[:, :, :], ALU.mult))
                    link(dve.tensor_reduce(cmax[:, :], cand[:, :, :], AX.X, ALU.max))
                    link(dve.tensor_tensor(rest[:, :, :], cand[:, :, :], over_experts(cmax), ALU.is_equal))
                    dve.tensor_tensor(sel[:, :, :, :].rearrange("p a b e -> p b a e"),
                                      sel1[:, :, :].rearrange("p (b a) e -> p b a e", a=TT),
                                      rest[:, :, :].rearrange("p (b a) e -> p b a e", a=TT), ALU.add).then_inc(sel_ready, 1)
                    dve.wait_ge(exp_ready, n + 1)
                    link(dve.tensor_reduce(esum[:, :], lexp[:, :, :], AX.X, ALU.add))
                    link(dve.reciprocal(cmax[:, :], esum[:, :]))
                    link(dve.scalar_tensor_tensor(out=prob[:, :, :], in0=lexp[:, :, :], scalar=0.5,
                                                  in1=over_experts(cmax), op0=ALU.mult, op1=ALU.mult))
                    link(dve.tensor_copy(p16[:, :, 0, :], prob[:, :, :]))
                    dve.tensor_tensor(p16[:, :, 1, :], prob[:, :, :], p16[:, :, 0, :], ALU.subtract).then_inc(prob_split, 1)
                elif kind == "ps":
                    wait_ready(dve, s)
                    dve.scalar_tensor_tensor(out=key[:, :, :, :].rearrange("p a b e -> p (a b e)"),
                                             in0=bank(s)[:, 0:GT * E], scalar=1.0,
                                             in1=sel[:, :, :, :].rearrange("p a b e -> p (a b e)"),
                                             op0=ALU.add, op1=ALU.mult).then_inc(taken(s), 1)
                    wait_taken(dve, s)
                    for i in range(GB):
                        dve.tensor_tensor(
                            oh[:, TT * i:TT * i + TT, 0:SLOTS].rearrange("p a (e c) -> p a e c", e=E),
                            iota[:, :].unsqueeze(1).unsqueeze(1).broadcast_to([P, TT, E, CAP]),
                            key[:, :, i, :].unsqueeze(3).broadcast_to([P, TT, E, CAP]),
                            ALU.is_equal).then_inc(oh_ready, 1)
                elif kind == "pw":
                    _, l, g = s
                    if n == 0:
                        dve.wait_ge(consts_made, 2)
                    wait_ready(dve, s)
                    pm = yp[:, 0, 0:GB * KT * 2 * E]
                    if n:
                        dve.wait_ge(yl_ready, before(s, "yt"))
                    dve.tensor_tensor(pm, bank(s)[:, 0:GB * KT * 2 * E], pmask[:, :], ALU.mult).then_inc(taken(s), 1)
                    wait_taken(dve, s)
                    link(dve.tensor_reduce(pslot[:, parity(l, g), :], pm.rearrange("p (s a) -> p s a", a=2 * E), AX.X, ALU.add))
                elif kind == "dpl":
                    _, l, g, i = s
                    wait_ready(dve, s)
                    dve.tensor_copy(xe[:, parity(l, g), 1, :, i * CAP:(i + 1) * CAP],
                                    bank(s)[:, 0:SLOTS].rearrange("p (e c) -> p e c", e=E)).then_inc(taken(s), 1)
                elif kind == "up":
                    _, l, g, e = s
                    if n == 0:
                        wait_taken(dve, ("bt",))
                    if n >= 2:
                        dve.wait_ge(y_ready, n - 1)
                    dve.wait_ge(h_ready, 2 * n + 2)
                    for c in range(2, 4):
                        ins = dve.tensor_scalar(hid[:, n % 2, c, :], psS[:, 2 * (n % 2) + 1, (c - 2) * GS:(c - 1) * GS],
                                                biasT[:, e * HC + c:e * HC + c + 1], 0.0, ALU.add, ALU.max)
                    ins.then_inc(h_dve, 1)
                elif kind == "yt":
                    _, l, g, i = s
                    wait_ready(dve, s)
                    if n >= 2:
                        dve.wait_ge(yl_ready, n - 1)
                    dve.tensor_tensor(yp[:, n % 2, :].rearrange("p (k c) -> p k c", k=KT),
                                      bank(s)[:, 0:SP_].rearrange("p (k c) -> p k c", k=KT),
                                      pslot[:, parity(l, g), KT * i:KT * i + KT].unsqueeze(2).broadcast_to([P, KT, C]),
                                      ALU.mult).then_inc(taken(s), 1)
                elif kind == "cb":
                    _, l, g, i = s
                    t = g * GT + 4 * i
                    wait_ready(dve, s)
                    xt = x[:, t:t + 4, :].rearrange("p t c -> p (t c)")
                    dve.tensor_tensor(xt, bank(s), xt, ALU.add).then_inc(taken(s), 1)
                elif kind == "qk":
                    _, p, w, c = s
                    dve.wait_ge(qk_hi, n + 1)
                    dve.scalar_tensor_tensor(out=qk16[:, w, c, 1, :], in0=bank(s), scalar=F ** -0.5 if w == 0 else 1.0,
                                             in1=qk16[:, w, c, 0, :], op0=ALU.mult, op1=ALU.subtract).then_inc(taken(s), 1)
                elif kind == "v":
                    b = s[1]
                    if n == 0:
                        dve.wait_ge(zeros_made, 2)
                    wait_ready(dve, s)
                    v = bank(s)[:, 0:T].rearrange("p (t h a d) -> p t h a d", t=TT, h=HEADS // 2, a=2)
                    for a in range(2):
                        c0 = a * (VW + HD)
                        ins = dve.tensor_copy(vst[:, b % 4, :, :, c0:c0 + HD], v[:, :, :, a, :])
                    ins.then_inc(taken(s), 1)
                elif kind == "xe":
                    _, b, half = s
                    dve.wait_ge(av_done, 4 * b + 2 * half + 2)
                    dve.tensor_copy(xy[:, b % 2, half, :], psY[:, half, 0:T]).then_inc(xy_taken, 1)
                elif kind == "ox":
                    wait_ready(dve, s)
                    r = bank(s).rearrange("p (g c) -> p g c", c=VW)
                    link(dve.tensor_scalar(den[:, :, :], r[:, :, 2 * HD:2 * HD + 2], DEN_EPS, None, ALU.add))
                    link(dve.reciprocal(rden[:, :, :], den[:, :, :]))
                    dve.tensor_tensor(onorm[:, :, :].rearrange("p t (g a d) -> p (t g) a d", a=2, d=HD),
                                      r[:, :, 0:2 * HD].rearrange("p g (a d) -> p g a d", a=2),
                                      rden[:, :, :].unsqueeze(3).broadcast_to([P, 16, 2, HD]), ALU.mult).then_inc(taken(s), 1)
                elif kind == "wo":
                    b = s[1]
                    wait_ready(dve, s)
                    xt = x[:, TT * b:TT * b + TT, :].rearrange("p t c -> p (t c)")
                    dve.tensor_tensor(xt, bank(s)[:, 0:T], xt, ALU.add).then_inc(taken(s), 1)

        @block.tensor
        def _(pe):
            mm = pe.matmul

            def take_bank(stage):
                k = item[stage]
                if k >= 2:
                    pe.wait_ge(bank_taken[k % 2], k // 2)

            def three(dst, lhs, rhs):
                mm(dst, lhs(0), rhs(0), start=True, stop=False)
                mm(dst, lhs(0), rhs(1), start=False, stop=False)
                return mm(dst, lhs(1), rhs(0), start=False, stop=True)

            pe.wait_ge(consts_made, 1)
            for s in ORDER:
                kind = s[0]
                n = nth[s]
                if kind in MISC:
                    take_bank(s)
                    m = bank(s)
                last = None
                if kind == "bt":
                    pe.wait_ge(bias_loaded, 32)
                    nb = E * HC + E
                    last = pe.transpose(m[:, 0:nb], bias_rows[:, :], ident[0:nb, 0:nb])
                elif kind == "xt":
                    pe.wait_ge(x_split, nth[("ln2",) + s[1:-1]] + 1)
                    src, q = (xf[:, parity(*s[2:4])], s[-1]) if s[1] == "f" else (xa[:, :, :, :], 0)
                    m16 = bank16(s)
                    for a in range(2):
                        for t in range(4):
                            o = (4 * a + t) * P
                            last = pe.transpose(m16[:, o:o + P], src[:, a, 4 * q + t, :], ident16[:, :])
                elif kind == "lg":
                    _, l, g = s
                    wait_taken(pe, ("xt", "f", l, g, 1))
                    wait_taken(pe, ("xt", "f", l, g, 0))
                    if n == 0:
                        pe.wait_ge(wsm_split, 1)
                    for t in range(GT):
                        for a in range(2):
                            last = mm(m[:, t * 2 * E:(t + 1) * 2 * E], xTf[:, a, t, :], wsm[:, :, WR],
                                      start=(a == 0), stop=(a == 1))
                elif kind == "ps":
                    pe.wait_ge(sel_ready, n + 1)
                    w = GB * E
                    mm(m[:, 0:w], upper16[:, :], sel[:, 0, :, :], start=True, stop=True)
                    mm(m[:, w:2 * w], ones16[:, :], sel[:, 0, :, :], start=True, stop=False)
                    last = mm(m[:, w:2 * w], upper16[:, :], sel[:, 1, :, :], start=False, stop=True)
                elif kind == "ot":
                    i = s[3]
                    pe.wait_ge(oh_ready, n + 1)
                    m16 = bank16(s)
                    for k in range(KT):
                        for t in range(TT):
                            o = (k * TT + t) * P
                            last = pe.transpose(m16[:, o:o + P], oh[:, TT * i + t, k * P:(k + 1) * P], ident16[:, :])
                elif kind == "pw":
                    pe.wait_ge(prob_split, n + 1)
                    for i in range(GB):
                        for k in range(KT):
                            o = (i * KT + k) * 2 * E
                            for t in range(TT):
                                last = mm(m[:, o:o + 2 * E], oh[:, TT * i + t, k * P:(k + 1) * P],
                                          p16[:, TT * i + t, :, :], start=(t == 0), stop=(t == TT - 1))
                elif kind in ("dph", "dpl"):
                    i = s[3]
                    for t in range(TT):
                        last = mm(m[:, 0:SLOTS], xf[:, parity(*s[1:3]), int(kind == "dpl"), TT * i + t, :], oh[:, TT * i + t, 0:SLOTS],
                                  start=(t == 0), stop=(t == TT - 1))
                elif kind == "up":
                    _, l, g, e = s
                    u = parity(l, g)
                    if e == 0:
                        for i in range(GB):
                            wait_taken(pe, ("dph", l, g, i))
                            wait_taken(pe, ("dpl", l, g, i))
                    if n < E:
                        pe.wait_ge(w1_split, e + 1)
                    if n >= 2:
                        pe.wait_ge(h_act, n - 1)
                        pe.wait_ge(h_dve, n - 1)
                    if before(s, "sc"):
                        pe.wait_ge(s_taken, before(s, "sc"))
                    for c in range(HC):
                        dst = psS[:, 2 * (n % 2) + c // 2, (c % 2) * GS:(c % 2 + 1) * GS]
                        ins = three(dst, lambda a: w1[:, a, e, c * P:(c + 1) * P], lambda a: xe[:, u, a, e, :])
                        if c % 2:
                            ins.then_inc(h_ready, 1)
                elif kind == "down":
                    _, l, g, e = s
                    pe.wait_ge(h_act, n + 1)
                    pe.wait_ge(h_dve, n + 1)
                    if n < E:
                        pe.wait_ge(w2_loaded[e], 16)
                    if n >= 2:
                        pe.wait_ge(y_taken, n - 1)
                    if before(s, "xe"):
                        pe.wait_ge(xy_taken, before(s, "xe"))
                    for c in range(HC):
                        ins = mm(psY[:, n % 2, 0:GS], w2[:, e, c, :], hid[:, n % 2, c, :], start=(c == 0), stop=(c == HC - 1))
                    ins.then_inc(y_ready, 1)
                elif kind == "yt":
                    _, l, g, i = s
                    pe.wait_ge(y_taken, nth[("down", l, g, E - 1)] + 1)
                    for k in range(KT):
                        last = pe.transpose(m[:, k * P:(k + 1) * P], yT[:, parity(l, g), i, k * P:(k + 1) * P], ident[:, :])
                elif kind == "cb":
                    _, l, g, i = s
                    pe.wait_ge(yl_ready, nth[("yt", l, g, 2 * i + 1)] + 1)
                    for j in range(4):
                        b, t = 2 * i + j // TT, j % TT
                        for k in range(KT):
                            for a in range(2):
                                last = mm(m[:, j * P:(j + 1) * P], ohT[:, parity(l, g), b, k, t * P:(t + 1) * P],
                                          y16[:, a, b, k * P:(k + 1) * P], start=(k + a == 0), stop=(k == KT - 1 and a == 1))
                elif kind == "qk":
                    _, p, w, c = s
                    wait_taken(pe, ("xt", "a", p, 0))
                    if n == 0:
                        pe.wait_ge(wsm_split, 2)
                    o = WQ[w] + c * P
                    last = three(m, lambda a: wsm[:, a, o:o + P],
                                 lambda a: xTa[:, a, :, :].rearrange("p t c -> p (t c)"))
                elif kind == "v":
                    for t in range(TT):
                        last = three(m[:, t * P:(t + 1) * P], lambda a: xTa[:, a, TT * (s[1] % 2) + t, :], lambda a: wsm[:, a, WV:WV + C])
                elif kind == "sc":
                    _, b, pair = s
                    if pair == 0:
                        pe.wait_ge(stack_loaded[b % 2], 8 * 16 * (b // 2 + 1))
                        if b == 0:
                            pe.wait_ge(zeros_made, 2)
                    if n >= 2:
                        pe.wait_ge(s_taken, n - 1)
                    else:
                        pe.wait_ge(h_act, before(s, "up"))
                        pe.wait_ge(h_dve, before(s, "up"))
                    for j in range(2):
                        h = HEAD_ORDER[2 * pair + j]
                        d = psS[:, 2 * (n % 2) + j, :]
                        q, k = stack[:, b % 2, 0, h, :], stack[:, b % 2, 1, h, :]
                        mm(d[:, P:P + T], k[:, 0:P], q, start=True, stop=True)
                        ins = mm(d[:, 0:P], k[:, P:T], q[:, P:T], start=True, stop=True)
                    ins.then_inc(s_ready, 1)
                elif kind == "av":
                    _, b, q = s
                    half = q // 2
                    if q == 0:
                        wait_taken(pe, ("v", b))
                    pe.wait_ge(a_ready, 2 * n + 2)
                    if q % 2 == 0:
                        if b:
                            pe.wait_ge(xy_taken, 2 * (b - 1) + half + 1)
                        else:
                            pe.wait_ge(y_taken, before(s, "down"))
                    for st in range(TT):
                        for j in range(4):
                            h = HEAD_ORDER[4 * q + j]
                            col = VW * ((h % 8) // 2)
                            a = amat[:, (2 * n + j // 2) % A_RING, j % 2, :]
                            v = vst[:, b % 4, st, h // 2, VW * (h % 2):VW * (h % 2) + VW]
                            if st == 0:
                                mm(psY[col:col + VW, half, 0:T], v, a[:, P:P + T], start=(q % 2 == 0), stop=False)
                            else:
                                ins = mm(psY[col:col + VW, half, P:T], v, a[:, 0:P], start=False, stop=(q % 2 == 1))
                    ins.then_inc(av_done, 1)
                elif kind == "ox":
                    b = s[1]
                    pe.wait_ge(xy_taken, 2 * b + 2)
                    for t in range(TT):
                        for half in range(2):
                            o = (2 * t + half) * P
                            last = pe.transpose(m[:, o:o + P], xy[:, b % 2, half, t * P:(t + 1) * P], ident[:, :])
                elif kind == "oT":
                    wait_taken(pe, ("ox", s[1]))
                    for t in range(TT):
                        last = pe.transpose(m[:, t * P:(t + 1) * P], onorm[:, t, :], ident[:, :])
                elif kind == "wo":
                    wait_taken(pe, ("oT", s[1]))
                    if n == 0:
                        pe.wait_ge(wo_loaded, 16)
                    for t in range(TT):
                        last = mm(m[:, t * P:(t + 1) * P], oT[:, t * P:(t + 1) * P], wo[:, :], start=True, stop=True)
                if kind in MISC:
                    last.then_inc(bank_ready[item[s] % 2], 1)


INPUTS = ["L0_attn_hidden_states", "L0_attn_Wq", "L0_attn_Wk", "L0_attn_Wv", "L0_attn_Wo",
          "L0_ffn_Wr", "L0_ffn_W1", "L0_ffn_b1", "L0_ffn_W2", "L0_ffn_b2"]


def kernel(**inputs):
    import numpy as np
    import concourse.bacc as bacc
    from concourse.bass_utils import run_bass_kernel_spmd

    nc = bacc.Bacc("TRN2", target_bir_lowering=False, num_devices=1)
    arrays, args = {}, []
    for name in INPUTS:
        a = np.ascontiguousarray(inputs[name])
        arrays[f"in_{name}"] = a
        args.append(nc.dram_tensor(f"in_{name}", a.shape, mybir.dt.from_np(a.dtype), kind="ExternalInput").ap())
    args.append(nc.dram_tensor("out", (B, T, C), mybir.dt.float32, kind="ExternalOutput").ap())
    macaron_program(nc, *args)
    return run_bass_kernel_spmd(nc, [arrays], core_ids=[0]).results[0]["out"]
```

```python
import concourse.bass as bass
from concourse import mybir
from contextlib import ExitStack

P = 128
B, T, C = 8, 256, 128
E, HID, K_TOP = 8, 512, 2
CAP = int(T / E * 1.25)
HEADS, F, HD = 16, 16, C // 16
TT = T // P
NT = B * TT
GB = 4
NG = B // GB
GT = GB * TT
SLOTS = E * CAP
KT = 3
SP_ = KT * P
GS = GB * CAP
HC = HID // P
NP = B // 2
PT = 2 * T
PTT = 2 * TT
LN_RING = 4
VW = 32
W1_RING = 7
LN_EPS = 1e-5
DEN_EPS = 1e-5
BIG = 1e30
HEAD_ORDER = [0, 2, 4, 6, 1, 3, 5, 7, 8, 10, 12, 14, 9, 11, 13, 15]
A_RING = 6
MISC = ("bt", "xt", "lg", "ps", "ot", "pw", "dph", "dpl", "yt", "cb", "qk", "v", "ox", "oT", "wo")


def weave(main, *sides):
    behind = [[] for _ in main]
    for start, every, stages in sides:
        for j, stage in enumerate(stages):
            behind[min(int(start + j * every), len(main) - 1)].append(stage)
    out = []
    for entry, extra in zip(main, behind):
        out += entry + extra
    return out


def stage_order():
    def norm(which, pair):
        return [("ln1", which, pair), ("ln2", which, pair)]

    def choose(l, g):
        return [("lg", l, g), ("c1", l, g), ("c2", l, g), ("sm", l, g), ("ps", l, g)]

    def spread(l, g):
        return [("ot", l, g, i) for i in range(GB)] + [("pw", l, g)]

    def dispatch(l, g):
        return [(kind, l, g, i) for i in range(GB) for kind in ("dph", "dpl")]

    def combine(l, g):
        yt, cb = ([(kind, l, g, i) for i in range(GB)] for kind in ("yt", "cb"))
        return [yt[0], yt[1], yt[2], cb[0], yt[3], cb[1], cb[2], cb[3]]

    def heads(p):
        return [("qk", p, w, c) for w in range(2) for c in range(2)]

    def experts(l, g):
        main = [[("up", l, g, 0)]]
        for e in range(E):
            if e + 1 < E:
                main.append([("up", l, g, e + 1)])
            main.append([("down", l, g, e)])
        return main

    order = [("bt",)]
    order += [("ln1", 0, 0), ("ln1", 0, 1), ("ln2", 0, 0), ("xt", 0, 0), ("ln2", 0, 1), ("xt", 0, 1)]
    order += choose(0, 0) + spread(0, 0) + [("ln1", 0, 2), ("ln1", 0, 3)] + dispatch(0, 0)
    order += weave(experts(0, 0), (0, 1, [("ln2", 0, 2), ("ln2", 0, 3)]), (2, 1, [("xt", 0, 2), ("xt", 0, 3)]),
                   (4, 1, choose(0, 1)), (10, .7, spread(0, 1)), (13, .4, dispatch(0, 1)))
    order += weave(experts(0, 1), (0, .8, combine(0, 0)), (6, 1, norm(1, 0)), (7, 1, [("xt", 1, 0)]), (8, 1, heads(0)),
                   (8, 1, norm(1, 1)), (12, 1, [("ld", 0), ("v", 0), ("v", 1), ("xt", 1, 1)]))
    main = []
    for n in range(B * HEADS // 2):
        main.append([("sc",) + divmod(n, HEADS // 2)])
        if n >= 3 and n % 2:
            b, q = divmod((n - 3) // 2, HEADS // 4)
            main[-1] += [("av", b, q)] + ([("xe", b, q // 2)] if q % 2 else [])
    sides = [(0, 1, [("ld", 1)]), (0, 1, heads(1)), (4, 1, [("v", 2), ("v", 3)]), (0, 1, combine(0, 1)),
             (6, 1, norm(1, 2)), (9, 1, [("xt", 1, 2)]), (10, 2, heads(2)), (10, 1, norm(1, 3)),
             (20, 1, [("xt", 1, 3)]), (22, 2, heads(3))]
    for b in range(B):
        if b >= 2:
            sides.append((8 * (b - 1) - 1, 1, [("ld", b)]))
        if b >= 4:
            sides.append((8 * (b - 3) + 2, 1, [("v", b)]))
        if b < B - 1:
            sides.append((8 * (b + 1) + 3, 2, [("ox", b), ("oT", b), ("wo", b)]))
    sides += [(25, 1, norm(2, 0)), (28, 1, [("xt", 2, 0)]), (40, 1, norm(2, 1)), (43, 1, [("xt", 2, 1)]),
              (44, 1, choose(1, 0)), (49, 1, spread(1, 0)), (55, 1, dispatch(1, 0)), (56, 1, norm(2, 2))]
    order += weave(main, *sides)
    order += [("av", B - 1, HEADS // 4 - 1), ("xe", B - 1, 1)]
    order += weave(experts(1, 0), (0, 1, [("ox", B - 1), ("oT", B - 1), ("wo", B - 1)]), (1, 1, [("xt", 2, 2)]),
                   (2, 1, norm(2, 3)), (5, 1, [("xt", 2, 3)]), (6, 1, choose(1, 1)), (11, .5, spread(1, 1)),
                   (13, .4, dispatch(1, 1)))
    order += weave(experts(1, 1), (0, .8, combine(1, 0)))
    order += combine(1, 1)
    return order


def macaron_program(nc, x_in, wq_in, wk_in, wv_in, wo_in, wr_in, w1_in, b1_in, w2_in, b2_in, out):
    f32, f16, i32 = mybir.dt.float32, mybir.dt.float16, mybir.dt.int32
    ALU, ACT, AX = mybir.AluOpType, mybir.ActivationFunctionType, mybir.AxisListType

    ORDER = stage_order()
    nth, seen, count_of = {}, {}, {}
    item = {}
    for s in ORDER:
        nth[s] = seen.get(s[0], 0)
        count_of[s] = dict(seen)
        seen[s[0]] = nth[s] + 1
        if s[0] in MISC:
            item[s] = len(item)

    def before(stage, kind):
        return count_of[stage].get(kind, 0)

    ctx = ExitStack()
    with ctx:
        def sb(name, shape, dt=f32):
            return ctx.enter_context(nc.sbuf_tensor(name, shape, dt))

        def sem(name):
            return ctx.enter_context(nc.semaphore(name))

        x = sb("x", [P, NT, C])
        stats = sb("stats", [P, LN_RING, PTT, 6])
        meanvar = sb("meanvar", [P, LN_RING, PTT, 2])
        std = sb("std", [P, LN_RING, PTT])
        rstd = sb("rstd", [P, LN_RING, PTT])
        xn = sb("xn", [P, PTT, C])
        xf = sb("xf", [P, 2, 2, GT, C], f16)
        xa = sb("xa", [P, 2, 4, C], f16)
        xTf = sb("xTf", [P, 2, GT, P], f16)
        xTa = sb("xTa", [P, 2, 4, P], f16)
        lg = sb("lg", [P, GT, E])
        lmax = sb("lmax", [P, GT])
        ldiff = sb("ldiff", [P, GT, E])
        lexp = sb("lexp", [P, GT, E])
        cand = sb("cand", [P, GT, E])
        cmax = sb("cmax", [P, GT])
        sel1 = sb("sel1", [P, GT, E])
        rest = sb("rest", [P, GT, E])
        esum = sb("esum", [P, GT])
        prob = sb("prob", [P, GT, E])
        p16 = sb("p16", [P, GT, 2, E], f16)
        sel = sb("sel", [P, TT, GB, E], f16)
        key = sb("key", [P, TT, GB, E])
        oh = sb("oh", [P, GT, SP_], f16)
        ohT = sb("ohT", [P, 2, GB, KT, T], f16)
        pmask = sb("pmask", [P, GB * KT * 2 * E])
        pslot = sb("pslot", [P, 2, GB * KT])
        xe = sb("xe", [P, 2, 2, E, GS], f16)
        hid = sb("hid", [P, 2, HC, GS])
        yT = sb("yT", [P, 2, GB, SP_])
        yp = sb("yp", [P, 2, SP_])
        y16 = sb("y16", [P, 2, GB, SP_], f16)
        w1 = sb("w1", [P, 2, E, HID], f16)
        w2 = sb("w2", [P, E, HC, C])
        bias_rows = sb("bias_rows", [E * HC + E, P])
        biasT = sb("biasT", [P, E * HC + E])
        wsm = sb("wsm", [P, 2, 8 + 3 * 256 - 128], f16)
        wo = sb("wo", [P, C])
        qk16 = sb("qk16", [P, 2, 2, 2, PT], f16)
        stack = sb("stack", [P, 2, 2, HEADS, T], f16)
        amat = sb("amat", [P, A_RING, 2, T + P])
        wsml = amat[:, 0, :, :].rearrange("p h c -> p (h c)")[:, 0:648]
        w1s = amat[:, 1:6, :, :].rearrange("p s h c -> p (s h c)")[:, 0:W1_RING * HID].rearrange("p (s c) -> p s c", c=HID)
        vst = sb("vst", [P, 4, TT, HEADS // 2, 2 * VW])
        xy = sb("xy", [P, 2, 2, T])
        den = sb("den", [P, 16, 2])
        rden = sb("rden", [P, 16, 2])
        onorm = sb("onorm", [P, TT, C])
        oT = sb("oT", [P, T])
        eps = sb("eps", [P, 1])
        warm = sb("warm", [P, 1])
        ident = sb("ident", [P, P])
        ident16 = sb("ident16", [P, P], f16)
        ones16 = sb("ones16", [P, P], f16)
        upper16 = sb("upper16", [P, P], f16)
        iota_i = sb("iota_i", [P, CAP], i32)
        iota = sb("iota", [P, CAP], f16)
        rank_i = sb("rank_i", [P, GT, E], i32)
        rank = sb("rank", [P, GT, E])

        psS = ctx.enter_context(nc.psum_tensor("psS", [P, 4, 512], f32))
        psY = ctx.enter_context(nc.psum_tensor("psY", [P, 2, 512], f32))
        psM = ctx.enter_context(nc.psum_tensor("psM", [P, 2, 512], f32))

        scr = nc.dram_tensor("qk_parts", [NP, 2, 2, HEADS * F, PT], f16, kind="Internal").ap()

        x_loaded = [sem(f"x_loaded{c}") for c in range(4)]
        wr_loaded, wqkv_loaded = sem("wr_loaded"), sem("wqkv_loaded")
        bias_loaded = sem("bias_loaded")
        w1_loaded = [sem(f"w1_loaded{c}") for c in range(E)]
        w2_loaded = [sem(f"w2_loaded{c}") for c in range(E)]
        wo_loaded = sem("wo_loaded")
        eps_made, consts_made = sem("eps_made"), sem("consts_made")
        zeros_made = sem("zeros_made")
        wsm_hi, wsm_split = sem("wsm_hi"), sem("wsm_split")
        w1_hi, w1_split = sem("w1_hi"), sem("w1_split")
        bank_ready = [sem(f"bank_ready{c}") for c in range(2)]
        bank_taken = [sem(f"bank_taken{c}") for c in range(2)]
        var_ready, std_ready, x_split = sem("var_ready"), sem("std_ready"), sem("x_split")
        diff_ready, exp_ready = sem("diff_ready"), sem("exp_ready")
        sel_ready, prob_split, oh_ready = sem("sel_ready"), sem("prob_split"), sem("oh_ready")
        h_ready, h_taken = sem("h_ready"), sem("h_taken")
        y_ready, y_taken = sem("y_ready"), sem("y_taken")
        yh_ready, yl_ready = sem("yh_ready"), sem("yl_ready")
        qk_hi = sem("qk_hi")
        qk_stored = [sem(f"qk_stored{c}") for c in range(4)]
        stack_loaded = [sem(f"stack_loaded{c}") for c in range(2)]
        s_ready, s_taken, a_ready = sem("s_ready"), sem("s_taken"), sem("a_ready")
        av_done, xy_taken = sem("av_done"), sem("xy_taken")
        dve_step, pool_step = sem("dve_step"), sem("pool_step")
        stored = sem("stored")

        def wait_ready(eng, stage):
            k = item[stage]
            eng.wait_ge(bank_ready[k % 2], k // 2 + 1)

        def wait_taken(eng, stage):
            k = item[stage]
            eng.wait_ge(bank_taken[k % 2], k // 2 + 1)

        def bank(stage):
            return psM[:, item[stage] % 2, :]

        def bank16(stage):
            return bank(stage).bitcast(f16)

        def taken(stage):
            return bank_taken[item[stage] % 2]

        def token_parts(which, p):
            if which == 1:
                return xa[:, :, :, :], xTa[:, :, :, :]
            q = slice(PTT * (p % 2), PTT * (p % 2 + 1))
            return xf[:, p // 2, :, q, :], xTf[:, :, q, :]

        def parity(l, g):
            return (l * NG + g) % 2

        WR, WQ, WV = slice(0, 8), (8, 264), 520

        block = ctx.enter_context(nc.Block())

        @block.sync
        def _(sp):
            for c in range(4):
                sp.dma_start(x[:, 4 * c:4 * c + 4, :],
                             x_in[2 * c:2 * c + 2].rearrange("b (t p) c -> p (b t) c", p=P)).then_inc(x_loaded[c], 16)
                if c == 0:
                    sp.dma_start(wsml[:, WR], wr_in).then_inc(wr_loaded, 16)
                    sp.dma_start(bias_rows[0:E * HC, :], b1_in.rearrange("e (h c) -> (e h) c", c=P)).then_inc(bias_loaded, 16)
                    sp.dma_start(bias_rows[E * HC:, :], b2_in).then_inc(bias_loaded, 16)
            sp.dma_start(wsml[:, 8:264], wq_in).then_inc(wqkv_loaded, 16)
            sp.dma_start(wsml[:, 264:520], wk_in).then_inc(wqkv_loaded, 16)
            sp.dma_start(wsml[:, 520:648], wv_in).then_inc(wqkv_loaded, 16)
            sp.dma_start(wo[:, :], wo_in).then_inc(wo_loaded, 16)
            for e in range(E):
                if e >= W1_RING:
                    sp.wait_ge(w1_split, e - W1_RING + 1)
                sp.dma_start(w1s[:, e % W1_RING, :], w1_in[e]).then_inc(w1_loaded[e], 16)
                sp.dma_start(w2[:, e, :, :], w2_in[e].rearrange("(h p) c -> p h c", p=P)).then_inc(w2_loaded[e], 16)
            n_stored = 0
            for s in ORDER:
                if s[0] == "qk":
                    _, p, w, c = s
                    wait_taken(sp, s)
                    sp.dma_start(scr[p, w, :, c * P:(c + 1) * P, :].rearrange("a r t -> r a t"),
                                 qk16[:, w, c, :, :]).then_inc(qk_stored[2 * w + c], 16)
                elif s[0] == "ld":
                    b = s[1]
                    p = b // 2
                    for c in range(4):
                        sp.wait_ge(qk_stored[c], 16 * (p + 1))
                    if b >= 2:
                        sp.wait_ge(s_ready, (b - 1) * HEADS // 2)
                    for w in range(2):
                        for r in range(4):
                            part = (r % 2) if w == 0 else (r // 2)
                            src = scr[p, w, part, :, (b % 2) * T:(b % 2 + 1) * T].rearrange("(h f) t -> f h t", f=F)
                            sp.dma_start(stack[r * F:(r + 1) * F, b % 2, w, :, :], src).then_inc(stack_loaded[b % 2], 16)
                elif s[0] == "cb" and s[1] == 1:
                    _, _, g, i = s
                    wait_taken(sp, s)
                    b = g * GB + i
                    sp.dma_start(out[b].rearrange("(t p) c -> p t c", p=P),
                                 x[:, TT * b:TT * b + TT, :]).then_inc(stored, 16)
                    n_stored += 1
            sp.wait_ge(stored, 16 * n_stored)

        @block.gpsimd
        def _(pool):
            steps = [0]

            def link(ins):
                steps[0] += 1
                ins.then_inc(pool_step, 1)
                pool.wait_ge(pool_step, steps[0])

            pool.memset(eps[:, :], LN_EPS).then_inc(eps_made, 1)
            pool.memset(ident16[:, :], 0.0)
            pool.memset(ones16[:, :], 1.0)
            pool.iota(iota_i[:, :], pattern=[[1, CAP]], base=1, channel_multiplier=0)
            pool.iota(rank_i[:, :, :], pattern=[[0, GT], [-1, E]], base=E, channel_multiplier=0)
            link(pool.memset(ident[:, :], 0.0))
            pool.affine_select(out=ident16[:, :], in_=ident16[:, :], pattern=[[-1, P]], compare_op=ALU.not_equal,
                               fill=1.0, base=0, channel_multiplier=1)
            pool.affine_select(out=ident[:, :], in_=ident[:, :], pattern=[[-1, P]], compare_op=ALU.not_equal,
                               fill=1.0, base=0, channel_multiplier=1)
            pool.affine_select(out=upper16[:, :], in_=ones16[:, :], pattern=[[1, P]], compare_op=ALU.is_gt,
                               fill=0.0, base=0, channel_multiplier=-1)
            pool.tensor_copy(iota[:, :], iota_i[:, :])
            pool.tensor_copy(rank[:, :, :], rank_i[:, :, :]).then_inc(consts_made, 1)
            pool.memset(oh[:, :, SLOTS:], 0.0)
            pm = pmask[:, :].rearrange("p (b k a e) -> p b k a e", b=GB, k=KT, a=2)
            link(pool.memset(pmask[:, :], 1.0))
            link(pool.affine_select(out=pm, in_=pm, pattern=[[0, GB], [P, KT], [0, 2], [-CAP, E]],
                                    compare_op=ALU.is_ge, fill=0.0, base=0, channel_multiplier=1))
            last = pool.affine_select(out=pm, in_=pm, pattern=[[0, GB], [-P, KT], [0, 2], [CAP, E]],
                                      compare_op=ALU.is_gt, fill=0.0, base=CAP, channel_multiplier=-1)
            last.then_inc(consts_made, 1)

            def split_small(n, cols):
                pool.wait_ge(wsm_hi, n)
                pool.tensor_tensor(wsm[:, 1, cols], wsml[:, cols], wsm[:, 0, cols], ALU.subtract).then_inc(wsm_split, 1)

            split_small(1, WR)
            for e in range(E):
                pool.wait_ge(w1_hi, e + 1)
                pool.tensor_tensor(w1[:, 1, e, :], w1s[:, e % W1_RING, :], w1[:, 0, e, :], ALU.subtract).then_inc(w1_split, 1)
            pool.memset(yT[:, :, :, SLOTS:], 0.0).then_inc(zeros_made, 1)
            split_small(2, slice(8, 648))
            pool.wait_ge(wsm_split, 2)
            link(pool.memset(stack[4 * F:, :, :, :, :], 0.0))
            link(pool.memset(vst[:, :, :, :, :], 0.0))
            pool.memset(vst[:, :, :, :, 2 * HD:2 * HD + 1], 1.0)
            pool.memset(vst[:, :, :, :, VW + 2 * HD + 1:VW + 2 * HD + 2], 1.0).then_inc(zeros_made, 1)
            for s in ORDER:
                if s[0] == "sc":
                    n = nth[s]
                    pool.wait_ge(s_taken, n + 1)
                    d = amat[:, n % A_RING, :, 0:2 * P].rearrange("p h (c t) -> p h c t", t=P)
                    pool.affine_select(out=d, in_=d, pattern=[[0, 2], [0, 2], [1, P]], compare_op=ALU.is_ge,
                                       fill=0.0, base=0, channel_multiplier=-1).then_inc(a_ready, 1)

        @block.scalar
        def _(act):
            act.wait_ge(eps_made, 1)
            act.activation(warm[:, :], eps[:, :], ACT.Sqrt)
            act.wait_ge(wr_loaded, 16)
            act.activation(wsm[:, 0, WR], wsml[:, WR], ACT.Copy).then_inc(wsm_hi, 1)

            def split_w1(e):
                act.wait_ge(w1_loaded[e], 16)
                act.activation(w1[:, 0, e, :], w1s[:, e % W1_RING, :], ACT.Copy).then_inc(w1_hi, 1)

            n_w1 = 0
            for s in ORDER:
                kind = s[0]
                n = nth[s]
                if kind == "ln1":
                    act.wait_ge(var_ready, n + 1)
                    act.activation(std[:, n % LN_RING, :], meanvar[:, n % LN_RING, :, 1], ACT.Sqrt,
                                   bias=eps[:, :]).then_inc(std_ready, 1)
                elif kind == "c1":
                    act.wait_ge(diff_ready, n + 1)
                    act.activation(lexp[:, :, :], ldiff[:, :, :], ACT.Exp).then_inc(exp_ready, 1)
                elif kind == "up":
                    _, l, g, e = s
                    if n >= 2:
                        act.wait_ge(y_ready, n - 1)
                    if n == 0:
                        wait_taken(act, ("bt",))
                    for c in range(HC):
                        if c % 2 == 0:
                            act.wait_ge(h_ready, 2 * n + c // 2 + 1)
                        ins = act.activation(hid[:, n % 2, c, :], psS[:, 2 * (n % 2) + c // 2, (c % 2) * GS:(c % 2 + 1) * GS],
                                             ACT.Relu, bias=biasT[:, e * HC + c:e * HC + c + 1])
                    ins.then_inc(h_taken, 1)
                elif kind == "down":
                    _, l, g, e = s
                    if n == 0:
                        act.wait_ge(zeros_made, 1)
                    act.wait_ge(y_ready, n + 1)
                    act.activation(yT[:, parity(l, g), :, e * CAP:(e + 1) * CAP],
                                   psY[:, n % 2, 0:GS].rearrange("p (b c) -> p b c", b=GB), ACT.Identity,
                                   bias=biasT[:, E * HC + e:E * HC + e + 1]).then_inc(y_taken, 1)
                elif kind == "yt":
                    i = s[3]
                    wait_taken(act, s)
                    act.activation(y16[:, 0, i, :], yp[:, n % 2, :], ACT.Copy).then_inc(yh_ready, 1)
                elif kind == "qk":
                    _, p, w, c = s
                    wait_ready(act, s)
                    if p:
                        act.wait_ge(qk_stored[2 * w + c], 16 * p)
                    act.activation(qk16[:, w, c, 0, :], bank(s), ACT.Copy, scale=F ** -0.5 if w == 0 else 1.0)\
                        .then_inc(qk_hi, 1)
                elif kind == "sc":
                    act.wait_ge(s_ready, n + 1)
                    if n >= A_RING:
                        act.wait_ge(av_done, (n - A_RING) // 2 + 1)
                    act.activation(amat[:, n % A_RING, :, :], psS[:, 2 * (n % 2):2 * (n % 2) + 2, 0:T + P], ACT.Square)\
                        .then_inc(s_taken, 1)
                elif kind == "oT":
                    wait_ready(act, s)
                    act.activation(oT[:, :], bank(s)[:, 0:T], ACT.Copy).then_inc(taken(s), 1)
                if s in (("ln1", 0, 1), ("c1", 0, 0), ("c2", 0, 0), ("sm", 0, 0), ("dph", 0, 0, 0)):
                    for _ in range(1 if s[0] == "ln1" else 2 if s[0] in ("c1", "c2") else 1):
                        split_w1(n_w1)
                        n_w1 += 1
                elif s == ("dph", 0, 0, 2):
                    split_w1(n_w1)
                    n_w1 += 1
                    act.wait_ge(wqkv_loaded, 48)
                    act.activation(wsm[:, 0, 8:648], wsml[:, 8:648], ACT.Copy).then_inc(wsm_hi, 1)
            assert n_w1 == E

        @block.vector
        def _(dve):
            steps = [0]

            def link(ins):
                steps[0] += 1
                ins.then_inc(dve_step, 1)
                dve.wait_ge(dve_step, steps[0])

            def over_experts(t):
                return t[:, :].unsqueeze(2).broadcast_to([P, GT, E])

            dve.wait_ge(consts_made, 1)
            for s in ORDER:
                kind = s[0]
                n = nth[s]
                if kind == "bt":
                    wait_ready(dve, s)
                    dve.tensor_copy(biasT[:, :], bank(s)[:, 0:E * HC + E]).then_inc(taken(s), 1)
                elif kind == "ln1":
                    _, which, p = s
                    if which == 0:
                        dve.wait_ge(x_loaded[p], 16)
                    else:
                        for b in (2 * p, 2 * p + 1):
                            wait_taken(dve, ("cb", 0, b // GB, b % GB) if which == 1 else ("wo", b))
                    for i in range(PTT):
                        ins = dve.bn_stats(stats[:, n % LN_RING, i, :], x[:, PTT * p + i, :])
                    link(ins)
                    for i in range(PTT):
                        ins = dve.bn_aggr(meanvar[:, n % LN_RING, i, :], stats[:, n % LN_RING, i, :])
                    ins.then_inc(var_ready, 1)
                elif kind == "ln2":
                    _, which, p = s
                    r = nth[("ln1",) + s[1:]] % LN_RING
                    dve.wait_ge(std_ready, nth[("ln1",) + s[1:]] + 1)
                    link(dve.reciprocal(rstd[:, r, :], std[:, r, :]))
                    for i in range(PTT):
                        ins = dve.tensor_scalar(xn[:, i, :], x[:, PTT * p + i, :], meanvar[:, r, i, 0:1],
                                                rstd[:, r, i:i + 1], ALU.subtract, ALU.mult)
                    link(ins)
                    parts = token_parts(which, p)[0]
                    if which == 1 and p:
                        wait_ready(dve, ("xt", 1, p - 1))
                    elif which == 2:
                        wait_ready(dve, ("dpl", 0, p // 2, GB - 1))
                    link(dve.tensor_copy(parts[:, 0], xn[:, :, :]))
                    dve.tensor_tensor(parts[:, 1], xn[:, :, :], parts[:, 0], ALU.subtract).then_inc(x_split, 1)
                elif kind == "xt":
                    dst = token_parts(*s[1:])[1]
                    wait_ready(dve, s)
                    dve.tensor_copy(dst.rearrange("p a t c -> p a (t c)"),
                                    bank16(s).rearrange("p (a n) -> p a n", a=2)).then_inc(taken(s), 1)
                elif kind == "lg":
                    wait_ready(dve, s)
                    dve.tensor_reduce(lg[:, :, :], bank(s)[:, 0:GT * 2 * E].rearrange("p (t a e) -> p t e a", t=GT, a=2),
                                      AX.X, ALU.add).then_inc(taken(s), 1)
                    wait_taken(dve, s)
                    link(dve.tensor_reduce(lmax[:, :], lg[:, :, :], AX.X, ALU.max))
                    dve.tensor_tensor(ldiff[:, :, :], lg[:, :, :], over_experts(lmax), ALU.subtract).then_inc(diff_ready, 1)
                elif kind == "c1":
                    dve.wait_ge(diff_ready, n + 1)
                    link(dve.scalar_tensor_tensor(out=cand[:, :, :], in0=ldiff[:, :, :], scalar=0.0, in1=rank[:, :, :],
                                                  op0=ALU.is_ge, op1=ALU.mult))
                    link(dve.tensor_reduce(cmax[:, :], cand[:, :, :], AX.X, ALU.max))
                    link(dve.tensor_tensor(sel1[:, :, :], cand[:, :, :], over_experts(cmax), ALU.is_equal))
                    link(dve.scalar_tensor_tensor(out=rest[:, :, :], in0=sel1[:, :, :], scalar=-BIG, in1=ldiff[:, :, :],
                                                  op0=ALU.mult, op1=ALU.add))
                elif kind == "c2":
                    link(dve.tensor_reduce(lmax[:, :], rest[:, :, :], AX.X, ALU.max))
                    link(dve.tensor_tensor(cand[:, :, :], rest[:, :, :], over_experts(lmax), ALU.is_ge))
                    link(dve.tensor_tensor(cand[:, :, :], cand[:, :, :], rank[:, :, :], ALU.mult))
                    link(dve.tensor_reduce(cmax[:, :], cand[:, :, :], AX.X, ALU.max))
                    link(dve.tensor_tensor(rest[:, :, :], cand[:, :, :], over_experts(cmax), ALU.is_equal))
                    dve.tensor_tensor(sel[:, :, :, :].rearrange("p a b e -> p b a e"),
                                      sel1[:, :, :].rearrange("p (b a) e -> p b a e", a=TT),
                                      rest[:, :, :].rearrange("p (b a) e -> p b a e", a=TT), ALU.add).then_inc(sel_ready, 1)
                elif kind == "sm":
                    dve.wait_ge(exp_ready, n + 1)
                    link(dve.tensor_reduce(esum[:, :], lexp[:, :, :], AX.X, ALU.add))
                    link(dve.reciprocal(cmax[:, :], esum[:, :]))
                    link(dve.scalar_tensor_tensor(out=prob[:, :, :], in0=lexp[:, :, :], scalar=0.5,
                                                  in1=over_experts(cmax), op0=ALU.mult, op1=ALU.mult))
                    link(dve.tensor_copy(p16[:, :, 0, :], prob[:, :, :]))
                    dve.tensor_tensor(p16[:, :, 1, :], prob[:, :, :], p16[:, :, 0, :], ALU.subtract).then_inc(prob_split, 1)
                elif kind == "ps":
                    wait_ready(dve, s)
                    dve.scalar_tensor_tensor(out=key[:, :, :, :].rearrange("p a b e -> p (a b e)"),
                                             in0=bank(s)[:, 0:GT * E], scalar=1.0,
                                             in1=sel[:, :, :, :].rearrange("p a b e -> p (a b e)"),
                                             op0=ALU.add, op1=ALU.mult).then_inc(taken(s), 1)
                    wait_taken(dve, s)
                    for i in range(GB):
                        dve.tensor_tensor(
                            oh[:, TT * i:TT * i + TT, 0:SLOTS].rearrange("p a (e c) -> p a e c", e=E),
                            iota[:, :].unsqueeze(1).unsqueeze(1).broadcast_to([P, TT, E, CAP]),
                            key[:, :, i, :].unsqueeze(3).broadcast_to([P, TT, E, CAP]),
                            ALU.is_equal).then_inc(oh_ready, 1)
                elif kind == "pw":
                    _, l, g = s
                    if n == 0:
                        dve.wait_ge(consts_made, 2)
                    wait_ready(dve, s)
                    pm = yp[:, 0, 0:GB * KT * 2 * E]
                    if before(s, "yt"):
                        dve.wait_ge(yl_ready, before(s, "yt"))
                    dve.tensor_tensor(pm, bank(s)[:, 0:GB * KT * 2 * E], pmask[:, :], ALU.mult).then_inc(taken(s), 1)
                    wait_taken(dve, s)
                    link(dve.tensor_reduce(pslot[:, parity(l, g), :], pm.rearrange("p (s a) -> p s a", a=2 * E), AX.X, ALU.add))
                elif kind == "ot":
                    _, l, g, i = s
                    wait_ready(dve, s)
                    dve.tensor_copy(ohT[:, parity(l, g), i, :, :].rearrange("p k t -> p (k t)"),
                                    bank16(s)[:, 0:KT * T]).then_inc(taken(s), 1)
                elif kind in ("dph", "dpl"):
                    _, l, g, i = s
                    wait_ready(dve, s)
                    dve.tensor_copy(xe[:, parity(l, g), int(kind == "dpl"), :, i * CAP:(i + 1) * CAP],
                                    bank(s)[:, 0:SLOTS].rearrange("p (e c) -> p e c", e=E)).then_inc(taken(s), 1)
                elif kind == "yt":
                    _, l, g, i = s
                    wait_ready(dve, s)
                    if n >= 2:
                        dve.wait_ge(yl_ready, n - 1)
                    u = parity(l, g)
                    dve.tensor_tensor(yp[:, n % 2, :].rearrange("p (k c) -> p k c", k=KT),
                                      bank(s)[:, 0:SP_].rearrange("p (k c) -> p k c", k=KT),
                                      pslot[:, u, KT * i:KT * i + KT].unsqueeze(2).broadcast_to([P, KT, C]),
                                      ALU.mult).then_inc(taken(s), 1)
                    dve.wait_ge(yh_ready, n + 1)
                    dve.tensor_tensor(y16[:, 1, i, :], yp[:, n % 2, :], y16[:, 0, i, :], ALU.subtract).then_inc(yl_ready, 1)
                elif kind == "cb":
                    _, l, g, i = s
                    t = g * GT + TT * i
                    wait_ready(dve, s)
                    xt = x[:, t:t + TT, :].rearrange("p t c -> p (t c)")
                    dve.tensor_tensor(xt, bank(s)[:, 0:T], xt, ALU.add).then_inc(taken(s), 1)
                elif kind == "qk":
                    _, p, w, c = s
                    dve.wait_ge(qk_hi, n + 1)
                    dve.scalar_tensor_tensor(out=qk16[:, w, c, 1, :], in0=bank(s), scalar=F ** -0.5 if w == 0 else 1.0,
                                             in1=qk16[:, w, c, 0, :], op0=ALU.mult, op1=ALU.subtract).then_inc(taken(s), 1)
                elif kind == "v":
                    b = s[1]
                    if n == 0:
                        dve.wait_ge(zeros_made, 2)
                    wait_ready(dve, s)
                    v = bank(s)[:, 0:T].rearrange("p (t h a d) -> p t h a d", t=TT, h=HEADS // 2, a=2)
                    for a in range(2):
                        c0 = a * (VW + HD)
                        ins = dve.tensor_copy(vst[:, b % 4, :, :, c0:c0 + HD], v[:, :, :, a, :])
                    ins.then_inc(taken(s), 1)
                elif kind == "xe":
                    _, b, half = s
                    dve.wait_ge(av_done, 4 * b + 2 * half + 2)
                    dve.tensor_copy(xy[:, b % 2, half, :], psY[:, half, 0:T]).then_inc(xy_taken, 1)
                elif kind == "ox":
                    wait_ready(dve, s)
                    r = bank(s).rearrange("p (g c) -> p g c", c=VW)
                    link(dve.tensor_scalar(den[:, :, :], r[:, :, 2 * HD:2 * HD + 2], DEN_EPS, None, ALU.add))
                    link(dve.reciprocal(rden[:, :, :], den[:, :, :]))
                    dve.tensor_tensor(onorm[:, :, :].rearrange("p t (g a d) -> p (t g) a d", a=2, d=HD),
                                      r[:, :, 0:2 * HD].rearrange("p g (a d) -> p g a d", a=2),
                                      rden[:, :, :].unsqueeze(3).broadcast_to([P, 16, 2, HD]), ALU.mult).then_inc(taken(s), 1)
                elif kind == "wo":
                    b = s[1]
                    wait_ready(dve, s)
                    xt = x[:, TT * b:TT * b + TT, :].rearrange("p t c -> p (t c)")
                    dve.tensor_tensor(xt, bank(s)[:, 0:T], xt, ALU.add).then_inc(taken(s), 1)

        @block.tensor
        def _(pe):
            mm = pe.matmul

            def take_bank(stage):
                k = item[stage]
                if k >= 2:
                    pe.wait_ge(bank_taken[k % 2], k // 2)

            def three(dst, lhs, rhs):
                mm(dst, lhs(0), rhs(0), start=True, stop=False)
                mm(dst, lhs(0), rhs(1), start=False, stop=False)
                return mm(dst, lhs(1), rhs(0), start=False, stop=True)

            pe.wait_ge(consts_made, 1)
            for s in ORDER:
                kind = s[0]
                n = nth[s]
                if kind in MISC:
                    take_bank(s)
                    m = bank(s)
                last = None
                if kind == "bt":
                    pe.wait_ge(bias_loaded, 32)
                    nb = E * HC + E
                    last = pe.transpose(m[:, 0:nb], bias_rows[:, :], ident[0:nb, 0:nb])
                elif kind == "xt":
                    pe.wait_ge(x_split, nth[("ln2",) + s[1:]] + 1)
                    src = token_parts(*s[1:])[0]
                    m16 = bank16(s)
                    for a in range(2):
                        for t in range(PTT):
                            o = (PTT * a + t) * P
                            last = pe.transpose(m16[:, o:o + P], src[:, a, t, :], ident16[:, :])
                elif kind == "lg":
                    _, l, g = s
                    wait_taken(pe, ("xt", 2 * l, 2 * g))
                    wait_taken(pe, ("xt", 2 * l, 2 * g + 1))
                    if n == 0:
                        pe.wait_ge(wsm_split, 1)
                    for t in range(GT):
                        for a in range(2):
                            last = mm(m[:, t * 2 * E:(t + 1) * 2 * E], xTf[:, a, t, :], wsm[:, :, WR],
                                      start=(a == 0), stop=(a == 1))
                elif kind == "ps":
                    pe.wait_ge(sel_ready, n + 1)
                    w = GB * E
                    mm(m[:, 0:w], upper16[:, :], sel[:, 0, :, :], start=True, stop=True)
                    mm(m[:, w:2 * w], ones16[:, :], sel[:, 0, :, :], start=True, stop=False)
                    last = mm(m[:, w:2 * w], upper16[:, :], sel[:, 1, :, :], start=False, stop=True)
                elif kind == "ot":
                    i = s[3]
                    pe.wait_ge(oh_ready, n + 1)
                    m16 = bank16(s)
                    for k in range(KT):
                        for t in range(TT):
                            o = (k * TT + t) * P
                            last = pe.transpose(m16[:, o:o + P], oh[:, TT * i + t, k * P:(k + 1) * P], ident16[:, :])
                elif kind == "pw":
                    pe.wait_ge(prob_split, n + 1)
                    for i in range(GB):
                        for k in range(KT):
                            o = (i * KT + k) * 2 * E
                            for t in range(TT):
                                last = mm(m[:, o:o + 2 * E], oh[:, TT * i + t, k * P:(k + 1) * P],
                                          p16[:, TT * i + t, :, :], start=(t == 0), stop=(t == TT - 1))
                elif kind in ("dph", "dpl"):
                    i = s[3]
                    for t in range(TT):
                        last = mm(m[:, 0:SLOTS], xf[:, parity(*s[1:3]), int(kind == "dpl"), TT * i + t, :], oh[:, TT * i + t, 0:SLOTS],
                                  start=(t == 0), stop=(t == TT - 1))
                elif kind == "up":
                    _, l, g, e = s
                    u = parity(l, g)
                    if e == 0:
                        for i in range(GB):
                            wait_taken(pe, ("dph", l, g, i))
                            wait_taken(pe, ("dpl", l, g, i))
                    if n < E:
                        pe.wait_ge(w1_split, e + 1)
                    if n >= 2:
                        pe.wait_ge(h_taken, n - 1)
                    if before(s, "sc"):
                        pe.wait_ge(s_taken, before(s, "sc"))
                    for c in range(HC):
                        dst = psS[:, 2 * (n % 2) + c // 2, (c % 2) * GS:(c % 2 + 1) * GS]
                        ins = three(dst, lambda a: w1[:, a, e, c * P:(c + 1) * P], lambda a: xe[:, u, a, e, :])
                        if c % 2:
                            ins.then_inc(h_ready, 1)
                elif kind == "down":
                    _, l, g, e = s
                    pe.wait_ge(h_taken, n + 1)
                    if n < E:
                        pe.wait_ge(w2_loaded[e], 16)
                    if n >= 2:
                        pe.wait_ge(y_taken, n - 1)
                    if before(s, "xe"):
                        pe.wait_ge(xy_taken, before(s, "xe"))
                    for c in range(HC):
                        ins = mm(psY[:, n % 2, 0:GS], w2[:, e, c, :], hid[:, n % 2, c, :], start=(c == 0), stop=(c == HC - 1))
                    ins.then_inc(y_ready, 1)
                elif kind == "yt":
                    _, l, g, i = s
                    pe.wait_ge(y_taken, nth[("down", l, g, E - 1)] + 1)
                    for k in range(KT):
                        last = pe.transpose(m[:, k * P:(k + 1) * P], yT[:, parity(l, g), i, k * P:(k + 1) * P], ident[:, :])
                elif kind == "cb":
                    _, l, g, i = s
                    pe.wait_ge(yl_ready, nth[("yt", l, g, i)] + 1)
                    for t in range(TT):
                        for k in range(KT):
                            for a in range(2):
                                last = mm(m[:, t * P:(t + 1) * P], ohT[:, parity(l, g), i, k, t * P:(t + 1) * P],
                                          y16[:, a, i, k * P:(k + 1) * P], start=(k + a == 0), stop=(k == KT - 1 and a == 1))
                elif kind == "qk":
                    _, p, w, c = s
                    wait_taken(pe, ("xt", 1, p))
                    if n == 0:
                        pe.wait_ge(wsm_split, 2)
                    o = WQ[w] + c * P
                    last = three(m, lambda a: wsm[:, a, o:o + P],
                                 lambda a: xTa[:, a, :, :].rearrange("p t c -> p (t c)"))
                elif kind == "v":
                    for t in range(TT):
                        last = three(m[:, t * P:(t + 1) * P], lambda a: xTa[:, a, TT * (s[1] % 2) + t, :], lambda a: wsm[:, a, WV:WV + C])
                elif kind == "sc":
                    _, b, pair = s
                    if pair == 0:
                        pe.wait_ge(stack_loaded[b % 2], 8 * 16 * (b // 2 + 1))
                        if b == 0:
                            pe.wait_ge(zeros_made, 2)
                    if n >= 2:
                        pe.wait_ge(s_taken, n - 1)
                    else:
                        pe.wait_ge(h_taken, before(s, "up"))
                    for j in range(2):
                        h = HEAD_ORDER[2 * pair + j]
                        d = psS[:, 2 * (n % 2) + j, :]
                        q, k = stack[:, b % 2, 0, h, :], stack[:, b % 2, 1, h, :]
                        mm(d[:, P:P + T], k[:, 0:P], q, start=True, stop=True)
                        ins = mm(d[:, 0:P], k[:, P:T], q[:, P:T], start=True, stop=True)
                    ins.then_inc(s_ready, 1)
                elif kind == "av":
                    _, b, q = s
                    half = q // 2
                    if q == 0:
                        wait_taken(pe, ("v", b))
                    pe.wait_ge(a_ready, 2 * n + 2)
                    if q % 2 == 0:
                        if b:
                            pe.wait_ge(xy_taken, 2 * (b - 1) + half + 1)
                        else:
                            pe.wait_ge(y_taken, before(s, "down"))
                    for st in range(TT):
                        for j in range(4):
                            h = HEAD_ORDER[4 * q + j]
                            col = VW * ((h % 8) // 2)
                            a = amat[:, (2 * n + j // 2) % A_RING, j % 2, :]
                            v = vst[:, b % 4, st, h // 2, VW * (h % 2):VW * (h % 2) + VW]
                            if st == 0:
                                mm(psY[col:col + VW, half, 0:T], v, a[:, P:P + T], start=(q % 2 == 0), stop=False)
                            else:
                                ins = mm(psY[col:col + VW, half, P:T], v, a[:, 0:P], start=False, stop=(q % 2 == 1))
                    ins.then_inc(av_done, 1)
                elif kind == "ox":
                    b = s[1]
                    pe.wait_ge(xy_taken, 2 * b + 2)
                    for t in range(TT):
                        for half in range(2):
                            o = (2 * t + half) * P
                            last = pe.transpose(m[:, o:o + P], xy[:, b % 2, half, t * P:(t + 1) * P], ident[:, :])
                elif kind == "oT":
                    wait_taken(pe, ("ox", s[1]))
                    for t in range(TT):
                        last = pe.transpose(m[:, t * P:(t + 1) * P], onorm[:, t, :], ident[:, :])
                elif kind == "wo":
                    wait_taken(pe, ("oT", s[1]))
                    if n == 0:
                        pe.wait_ge(wo_loaded, 16)
                    for t in range(TT):
                        last = mm(m[:, t * P:(t + 1) * P], oT[:, t * P:(t + 1) * P], wo[:, :], start=True, stop=True)
                if kind in MISC:
                    last.then_inc(bank_ready[item[s] % 2], 1)


INPUTS = ["L0_attn_hidden_states", "L0_attn_Wq", "L0_attn_Wk", "L0_attn_Wv", "L0_attn_Wo",
          "L0_ffn_Wr", "L0_ffn_W1", "L0_ffn_b1", "L0_ffn_W2", "L0_ffn_b2"]


def kernel(**inputs):
    import numpy as np
    import concourse.bacc as bacc
    from concourse.bass_utils import run_bass_kernel_spmd

    nc = bacc.Bacc("TRN2", target_bir_lowering=False, num_devices=1)
    arrays, args = {}, []
    for name in INPUTS:
        a = np.ascontiguousarray(inputs[name])
        arrays[f"in_{name}"] = a
        args.append(nc.dram_tensor(f"in_{name}", a.shape, mybir.dt.from_np(a.dtype), kind="ExternalInput").ap())
    args.append(nc.dram_tensor("out", (B, T, C), mybir.dt.float32, kind="ExternalOutput").ap())
    macaron_program(nc, *args)
    return run_bass_kernel_spmd(nc, [arrays], core_ids=[0]).results[0]["out"]
```

```python
import concourse.bass as bass
from concourse import mybir
from contextlib import ExitStack

P = 128
B, T, C = 8, 256, 128
E, HID, K_TOP = 8, 512, 2
CAP = int(T / E * 1.25)
HEADS, F, HD = 16, 16, C // 16
TT = T // P
NT = B * TT
GB = 4
NG = B // GB
GT = GB * TT
SLOTS = E * CAP
KT = 3
SP_ = KT * P
GS = GB * CAP
HC = HID // P
NP = B // 2
PT = 2 * T
PTT = 2 * TT
LN_RING = 4
VW = 32
W1_RING = 7
WARM_UP = 64
LN_EPS = 1e-5
DEN_EPS = 1e-5
BIG = 1e30
HEAD_ORDER = [0, 2, 4, 6, 1, 3, 5, 7, 8, 10, 12, 14, 9, 11, 13, 15]
A_RING = 6
ON_SCALAR = {("dph", 0, 0), ("dph", 0, 1), ("dph", 1, 0), ("dph", 1, 1), ("dpl", 0, 0), ("dpl", 1, 0),
             ("ot", 1, 0), ("v", 1), ("v", 2), ("v", 3), ("v", 6), ("v", 7),
             ("xe", 0), ("xe", 1), ("xe", 3), ("xe", 4), ("xe", 5)}
SPLIT_BEHIND = {("ln1", 0, 1): 1, ("c1", 0, 0): 2, ("ps", 0, 0): 3, ("up", 0, 0, 0): 1, ("up", 0, 0, 1): 1}
MISC = ("bt", "xt", "lg", "ps", "ot", "pw", "dph", "dpl", "yt", "cb", "qk", "v", "ox", "oT", "wo")


def weave(main, *sides):
    behind = [[] for _ in main]
    for start, every, stages in sides:
        for j, stage in enumerate(stages):
            behind[min(int(start + j * every), len(main) - 1)].append(stage)
    out = []
    for entry, extra in zip(main, behind):
        out += entry + extra
    return out


def stage_order():
    def norm(which, pair):
        return [("ln1", which, pair), ("lnx", which, pair), ("ln2", which, pair)]

    def choose(l, g):
        return [("lg", l, g, 1), ("c1", l, g), ("c2", l, g), ("ps", l, g)]

    def spread(l, g):
        return [("sm", l, g), ("pw", l, g)] + [("ot", l, g, i) for i in range(GB)]

    def dispatch(l, g):
        return [(kind, l, g, i) for i in range(GB) for kind in ("dph", "dpl")]

    def combine(l, g):
        cb = [("cb", l, g, i) for i in range(GB)]
        if (l, g) == (1, NG - 1):
            return [("yt", l, g, 1), ("yt", l, g, 2), ("yl", l, g, 1), ("yt", l, g, 3), ("ca", l, g),
                    ("yl", l, g, 2), ("yl", l, g, 3)] + cb
        return [("yt", l, g, 1), ("yt", l, g, 2), ("yl", l, g, 1), ("yl", l, g, 2)] + cb

    def weigh(l, g):
        return [("yt", l, g, 0), ("yl", l, g, 0)]

    def heads(p):
        return [("qk", p, w, c) for w in range(2) for c in range(2)]

    def experts(l, g):
        main = [[("up", l, g, 0)]]
        for e in range(E):
            if e + 1 < E:
                main.append([("up", l, g, e + 1)])
            main.append([("down", l, g, e)])
        return main

    order = [("ln1", 0, 0), ("ln1", 0, 1), ("lnx", 0, 0), ("ln2", 0, 0), ("xt", 0, 0), ("lnx", 0, 1), ("ln2", 0, 1),
        ("lg", 0, 0, 0), ("warm", 16, 0),
             ("xt", 0, 1), ("bt",)]
    c, d = choose(0, 0), dispatch(0, 0)
    order += c[:3] + [("warm", 30, 1), c[3], ("warm", 8, 2)] + weave([[x] for x in d], (4, 1, norm(0, 2)))
    order += weave(experts(0, 0), (.5, .5, norm(0, 3)), (0, 1, [("xt", 0, 2), ("lg", 0, 1, 0)]), (3.5, 1, [("xt", 0, 3)]),
                   (4.5, 1, choose(0, 1)), (4.5, 2, [("ex", 0, 0), ("ex", 0, 1), ("sq", 0)]),
                   (11, 1, spread(0, 0)[:1]), (8, 1, dispatch(0, 1)), (12, 1, spread(0, 0)[1:4]),
                   (22, 0, [("yt", 0, 0, 0), ("ot", 0, 0, 2), ("yl", 0, 0, 0), ("ot", 0, 0, 3)]))
    order += weave(experts(0, 1), (0, .5, combine(0, 0)), (2.5, 1, norm(1, 0)), (7.5, .5, [("xt", 1, 0)]), (8, .5, heads(0)),
                   (6.5, 2, spread(0, 1)[:1]), (12, 0, [("ld", 0)]), (10.5, .5, spread(0, 1)[1:]), (14, 1, weigh(0, 1)),
                   (10.5, 1, norm(1, 1)), (14.5, 1.5, [("v", 0), ("v", 1), ("xt", 1, 1)]))
    main = []
    for n in range(B * HEADS // 2):
        main.append([("sc",) + divmod(n, HEADS // 2)])
        if n >= 3 and n % 2:
            b, q = divmod((n - 3) // 2, HEADS // 4)
            main[-1] += [("av", b, q)] + ([("xe", b, q // 2)] if q % 2 else [])
    sides = [(1, 1.5, [("ld", 1)]), (0, 1, combine(0, 1)), (1, 1, heads(1)), (5.5, 2, [("v", 2), ("v", 3)]),
             (5, 1, norm(1, 2)), (10.5, 2, [("xt", 1, 2)]), (11.5, 2, heads(2)), (9, 1.5, norm(1, 3)),
             (21, .7, [("xt", 1, 3)]), (23, 2, heads(3))]
    for b in range(B):
        if b >= 2:
            sides.append((8 * (b - 1) - 2.5, 1, [("ld", b)]))
        if b >= 4:
            sides.append((8 * (b - 3) + 2.5, 0, [("v", b)]))
        if b < B - 1:
            sides.append((8 * (b + 1) + 3, 2, [("ox", b), ("oT", b), ("wo", b)]))
    sides += [(26.5, 1.5, norm(2, 0)), (36, 1, [("xt", 2, 0), ("lg", 1, 0, 0)]), (41, 1.5, norm(2, 1)),
              (46, .5, [("xt", 2, 1)]), (48.5, 1, choose(1, 0)), (54, .7, dispatch(1, 0)),
              (58.5, 2, norm(2, 2) + [("ex", 1, 0), ("sq", 1)])]
    order += weave(main, *sides)
    main = experts(1, 0)
    order += main[0] + [("av", B - 1, HEADS // 4 - 1), ("xe", B - 1, 1)]
    main[0] = []
    order += weave(main, (1.5, 1.5, [("sm", 1, 0)]), (.5, 1, [("ox", B - 1), ("oT", B - 1), ("wo", B - 1)]),
                   (0, 1, [("xt", 2, 2)]), (3, 1, norm(2, 3)), (3, 1, [("lg", 1, 1, 0)] + spread(1, 0)[1:]),
                   (6, .7, [("xt", 2, 3)]), (7, 1, choose(1, 1)),
                   (10, 2, [("ex", 1, 1)]), (12, .5, dispatch(1, 1)), (15.5, 2, weigh(1, 0)))
    order += weave(experts(1, 1), (0, 1.5, combine(1, 0)), (3.5, 1, spread(1, 1)), (13, 1.5, weigh(1, 1)))
    order += combine(1, 1)
    return order


def macaron_program(nc, x_in, wq_in, wk_in, wv_in, wo_in, wr_in, w1_in, b1_in, w2_in, b2_in, out):
    f32, f16, i32 = mybir.dt.float32, mybir.dt.float16, mybir.dt.int32
    ALU, ACT, AX = mybir.AluOpType, mybir.ActivationFunctionType, mybir.AxisListType

    ORDER = stage_order()
    nth, seen, count_of = {}, {}, {}
    item = {}
    for s in ORDER:
        nth[s] = seen.get(s[0], 0)
        count_of[s] = dict(seen)
        seen[s[0]] = nth[s] + 1
        if s[0] in MISC:
            item[s] = len(item)

    def before(stage, kind):
        return count_of[stage].get(kind, 0)

    ctx = ExitStack()
    with ctx:
        def sb(name, shape, dt=f32):
            return ctx.enter_context(nc.sbuf_tensor(name, shape, dt))

        def sem(name):
            return ctx.enter_context(nc.semaphore(name))

        x = sb("x", [P, NT, C])
        stats = sb("stats", [P, LN_RING, PTT, 6])
        meanvar = sb("meanvar", [P, LN_RING, PTT, 2])
        std = sb("std", [P, LN_RING, PTT])
        rstd = sb("rstd", [P, LN_RING, PTT])
        xn = sb("xn", [P, PTT, C])
        xf = sb("xf", [P, 2, 2, GT, C], f16)
        xa = sb("xa", [P, 2, 4, C], f16)
        xTf = sb("xTf", [P, 2, GT, P], f16)
        xTa = sb("xTa", [P, 2, 4, P], f16)
        lg = sb("lg", [P, GT, E])
        lmax = sb("lmax", [P, GT])
        ldiff = sb("ldiff", [P, 2, GT, E])
        cand = sb("cand", [P, GT, E])
        cmax = sb("cmax", [P, GT])
        sel1 = sb("sel1", [P, GT, E])
        rest = sb("rest", [P, GT, E])
        esum = sb("esum", [P, GT])
        prob = sb("prob", [P, GT, E])
        p16 = sb("p16", [P, GT, 2, E], f16)
        sel = sb("sel", [P, TT, GB, E], f16)
        key = sb("key", [P, TT, GB, E])
        oh = sb("oh", [P, 2, GT, SP_], f16)
        ohT = sb("ohT", [P, 2, GB, KT, T], f16)
        pmask = sb("pmask", [P, GB * KT * 2 * E])
        pslot = sb("pslot", [P, 2, GB * KT])
        xe = sb("xe", [P, 2, 2, E, GS], f16)
        hid = sb("hid", [P, 2, HC, GS])
        bias_rows = hid[0:E * HC + E, 1, 0, 0:P]
        yT = sb("yT", [P, 2, GB, SP_])
        yp = sb("yp", [P, 2, GB * P])
        y16 = sb("y16", [P, 2, GB, SP_], f16)
        w1 = sb("w1", [P, 2, E, HID], f16)
        w2 = sb("w2", [P, E, HC, C])
        biasT = sb("biasT", [P, E * HC + E])
        wsm = sb("wsm", [P, 2, 8 + 3 * 256 - 128], f16)
        wo = sb("wo", [P, C])
        qk16 = sb("qk16", [P, 2, 2, 2, PT], f16)
        stack = sb("stack", [P, 2, 2, HEADS, T], f16)
        amat = sb("amat", [P, A_RING, 2, T + P])
        wsml = amat[:, 0, :, :].rearrange("p h c -> p (h c)")[:, 0:648]
        w1s = amat[:, 1:6, :, :].rearrange("p s h c -> p (s h c)")[:, 0:W1_RING * HID].rearrange("p (s c) -> p s c", c=HID)
        vst = sb("vst", [P, 4, TT, HEADS // 2, 2 * VW])
        xy = sb("xy", [P, 2, 2, T])
        den = sb("den", [P, 16, 2])
        rden = sb("rden", [P, 16, 2])
        onorm = sb("onorm", [P, TT, C])
        oT = sb("oT", [P, T])
        eps = sb("eps", [P, 1])
        warm = sb("warm", [P, 1])
        ident = sb("ident", [P, P])
        ident16 = sb("ident16", [P, P], f16)
        ones16 = sb("ones16", [P, P], f16)
        upper16 = sb("upper16", [P, P], f16)
        iota = sb("iota", [P, CAP], f16)
        rank = sb("rank", [P, E])
        iota_i = cand[:, :, :].rearrange("p t e -> p (t e)")[:, 0:CAP].bitcast(i32)
        rank_i = rest[:, 0, :].bitcast(i32)

        psS = ctx.enter_context(nc.psum_tensor("psS", [P, 4, 512], f32))
        psY = ctx.enter_context(nc.psum_tensor("psY", [P, 2, 512], f32))
        psM = ctx.enter_context(nc.psum_tensor("psM", [P, 2, 512], f32))

        scr = nc.dram_tensor("qk_parts", [NP, 2, 2, HEADS * F, PT], f16, kind="Internal").ap()

        x_loaded = [sem(f"x_loaded{c}") for c in range(4)]
        wr_loaded, wqkv_loaded = sem("wr_loaded"), sem("wqkv_loaded")
        bias_loaded = sem("bias_loaded")
        w1_loaded = [sem(f"w1_loaded{c}") for c in range(E)]
        w2_loaded = [sem(f"w2_loaded{c}") for c in range(E)]
        wo_loaded = sem("wo_loaded")
        eps_made, ones_made, consts_made = sem("eps_made"), sem("ones_made"), sem("consts_made")
        zeros_made = sem("zeros_made")
        wsm_hi, wsm_split = sem("wsm_hi"), sem("wsm_split")
        w1_hi, w1_split = sem("w1_hi"), sem("w1_split")
        bank_ready = [sem(f"bank_ready{c}") for c in range(2)]
        bank_taken = [sem(f"bank_taken{c}") for c in range(2)]
        var_ready, std_ready, x_split = sem("var_ready"), sem("std_ready"), sem("x_split")
        diff_ready, exp_ready = sem("diff_ready"), sem("exp_ready")
        sel_ready, prob_split, oh_ready = sem("sel_ready"), sem("prob_split"), sem("oh_ready")
        h_ready, h_taken = sem("h_ready"), sem("h_taken")
        y_ready, y_taken = sem("y_ready"), sem("y_taken")
        yh_ready, yl_ready = sem("yh_ready"), sem("yl_ready")
        qk_hi = sem("qk_hi")
        qk_stored = [sem(f"qk_stored{c}") for c in range(4)]
        stack_loaded = [sem(f"stack_loaded{c}") for c in range(2)]
        s_ready, s_taken, a_ready = sem("s_ready"), sem("s_taken"), sem("a_ready")
        av_done, xy_taken = sem("av_done"), sem("xy_taken")
        dve_step, pool_step = sem("dve_step"), sem("pool_step")
        stored = sem("stored")

        units = [(l, g) for l in range(2) for g in range(NG)]

        def wait_ready(eng, stage):
            k = item[stage]
            eng.wait_ge(bank_ready[k % 2], k // 2 + 1)

        def wait_taken(eng, stage):
            k = item[stage]
            eng.wait_ge(bank_taken[k % 2], k // 2 + 1)

        def by_scalar(stage):
            return (stage[:2] if stage[0] in ("v", "xe") else stage[:3]) in ON_SCALAR

        def move(eng, dst, src):
            if eng is nc.scalar:
                return eng.activation(dst, src, ACT.Copy)
            return eng.tensor_copy(dst, src)

        def move_out(eng, s):
            kind, n = s[0], nth[s]
            if kind == "ot":
                _, l, g, i = s
                if l:
                    wait_ready(eng, ("cb", l - 1, g, GB - 1))
                wait_ready(eng, s)
                move(eng, ohT[:, parity(l, g), i, :, :].rearrange("p k t -> p (k t)"),
                     bank16(s)[:, 0:KT * T]).then_inc(taken(s), 1)
            elif kind in ("dph", "dpl"):
                _, l, g, i = s
                wait_ready(eng, s)
                move(eng, xe[:, parity(l, g), int(kind == "dpl"), :, i * CAP:(i + 1) * CAP],
                     bank(s)[:, 0:SLOTS].rearrange("p (e c) -> p e c", e=E)).then_inc(taken(s), 1)
            elif kind == "v":
                b = s[1]
                if b < 4:
                    eng.wait_ge(zeros_made, 2)
                if b >= 4:
                    eng.wait_ge(av_done, 4 * (b - 3))
                wait_ready(eng, s)
                v = bank(s)[:, 0:T].rearrange("p (t h a d) -> p t h a d", t=TT, h=HEADS // 2, a=2)
                for a in range(2):
                    c0 = a * (VW + HD)
                    ins = move(eng, vst[:, b % 4, :, :, c0:c0 + HD], v[:, :, :, a, :])
                ins.then_inc(taken(s), 1)
            elif kind == "xe":
                _, b, half = s
                if b >= 2:
                    wait_ready(eng, ("ox", b - 2))
                eng.wait_ge(av_done, 4 * b + 2 * half + 2)
                move(eng, xy[:, b % 2, half, :], psY[:, half, 0:T]).then_inc(xy_taken, 1)

        def last_unit(stage):
            return stage[0] == "cb" and stage[1:3] == units[-1]

        def weighted(stage):
            _, l, g, k = stage
            if (l, g) == units[-1] and k >= KT - 1:
                half = k - (KT - 1)
                return KT - 1, slice(half * GB // 2, (half + 1) * GB // 2)
            return k, slice(0, GB)

        def weighted_in(stage):
            k, rows = weighted(stage)
            w = (rows.stop - rows.start) * P
            return (yp[:, nth[stage] % 2, 0:w].rearrange("p (b c) -> p b c", c=C),
                    y16[:, 0, rows, k * P:(k + 1) * P], y16[:, 1, rows, k * P:(k + 1) * P])

        def bank(stage):
            return psS[:, stage[3], :] if last_unit(stage) else psM[:, item[stage] % 2, :]

        def bank16(stage):
            return bank(stage).bitcast(f16)

        def taken(stage):
            return bank_taken[item[stage] % 2]

        def token_parts(which, p):
            if which == 1:
                return xa[:, :, :, :], xTa[:, :, :, :]
            q = slice(PTT * (p % 2), PTT * (p % 2 + 1))
            return xf[:, p // 2, :, q, :], xTf[:, :, q, :]

        def parity(l, g):
            return (l * NG + g) % 2

        WR, WQ, WV = slice(0, 8), (8, 264), 520

        block = ctx.enter_context(nc.Block())

        @block.sync
        def _(sp):
            for c in range(4):
                sp.dma_start(x[:, 4 * c:4 * c + 4, :],
                             x_in[2 * c:2 * c + 2].rearrange("b (t p) c -> p (b t) c", p=P)).then_inc(x_loaded[c], 16)
                if c == 1:
                    sp.dma_start(wsml[:, WR], wr_in).then_inc(wr_loaded, 16)
                    sp.dma_start(bias_rows[0:E * HC], b1_in.rearrange("e (h c) -> (e h) c", c=P)).then_inc(bias_loaded, 16)
                    sp.dma_start(bias_rows[E * HC:], b2_in).then_inc(bias_loaded, 16)
            sp.dma_start(wsml[:, 8:264], wq_in).then_inc(wqkv_loaded, 16)
            sp.dma_start(wsml[:, 264:520], wk_in).then_inc(wqkv_loaded, 16)
            sp.dma_start(wsml[:, 520:648], wv_in).then_inc(wqkv_loaded, 16)
            sp.dma_start(wo[:, :], wo_in).then_inc(wo_loaded, 16)
            for e in range(E):
                if e >= W1_RING:
                    sp.wait_ge(w1_split, e - W1_RING + 1)
                sp.dma_start(w1s[:, e % W1_RING, :], w1_in[e]).then_inc(w1_loaded[e], 16)
                sp.dma_start(w2[:, e, :, :], w2_in[e].rearrange("(h p) c -> p h c", p=P)).then_inc(w2_loaded[e], 16)
            n_stored = 0
            for s in ORDER:
                if s[0] == "qk":
                    _, p, w, c = s
                    wait_taken(sp, s)
                    sp.dma_start(scr[p, w, :, c * P:(c + 1) * P, :].rearrange("a r t -> r a t"),
                                 qk16[:, w, c, :, :]).then_inc(qk_stored[2 * w + c], 16)
                elif s[0] == "ld":
                    b = s[1]
                    p = b // 2
                    for c in range(4):
                        sp.wait_ge(qk_stored[c], 16 * (p + 1))
                    if b >= 2:
                        sp.wait_ge(s_ready, (b - 1) * HEADS // 2)
                    for w, r, part, np_ in ((0, 0, 0, 2), (0, 2, 0, 2), (1, 0, 0, 2), (1, 2, 1, 1), (1, 3, 0, 1)):
                        src = scr[p, w, part:part + np_, :, (b % 2) * T:(b % 2 + 1) * T].rearrange("a (f h) t -> (a f) h t", f=F)
                        sp.dma_start(stack[r * F:(r + np_) * F, b % 2, w, :, :], src).then_inc(stack_loaded[b % 2], 16)
                elif s[0] == "cb" and s[1] == 1:
                    _, _, g, i = s
                    wait_taken(sp, s)
                    b = g * GB + i
                    sp.dma_start(out[b].rearrange("(t p) c -> p t c", p=P),
                                 x[:, TT * b:TT * b + TT, :]).then_inc(stored, 16)
                    n_stored += 1
            sp.wait_ge(stored, 16 * n_stored)

        @block.gpsimd
        def _(pool):
            steps = [0]

            def link(ins):
                steps[0] += 1
                ins.then_inc(pool_step, 1)
                pool.wait_ge(pool_step, steps[0])

            pool.memset(eps[:, :], LN_EPS).then_inc(eps_made, 1)
            pool.memset(ident16[:, :], 0.0)
            pool.memset(ones16[:, :], 1.0).then_inc(ones_made, 1)
            pool.iota(iota_i, pattern=[[1, CAP]], base=1, channel_multiplier=0)
            pool.iota(rank_i, pattern=[[-1, E]], base=E, channel_multiplier=0)
            link(pool.memset(ident[:, :], 0.0))
            pool.affine_select(out=ident16[:, :], in_=ident16[:, :], pattern=[[-1, P]], compare_op=ALU.not_equal,
                               fill=1.0, base=0, channel_multiplier=1)
            pool.affine_select(out=ident[:, :], in_=ident[:, :], pattern=[[-1, P]], compare_op=ALU.not_equal,
                               fill=1.0, base=0, channel_multiplier=1)
            pool.affine_select(out=upper16[:, :], in_=ones16[:, :], pattern=[[1, P]], compare_op=ALU.is_gt,
                               fill=0.0, base=0, channel_multiplier=-1)
            pool.tensor_copy(iota[:, :], iota_i)
            pool.tensor_copy(rank[:, :], rank_i).then_inc(consts_made, 1)
            pool.memset(oh[:, :, :, SLOTS:], 0.0)
            pm = pmask[:, :].rearrange("p (b k a e) -> p b k a e", b=GB, k=KT, a=2)
            link(pool.memset(pmask[:, :], 1.0))
            link(pool.affine_select(out=pm, in_=pm, pattern=[[0, GB], [P, KT], [0, 2], [-CAP, E]],
                                    compare_op=ALU.is_ge, fill=0.0, base=0, channel_multiplier=1))
            last = pool.affine_select(out=pm, in_=pm, pattern=[[0, GB], [-P, KT], [0, 2], [CAP, E]],
                                      compare_op=ALU.is_gt, fill=0.0, base=CAP, channel_multiplier=-1)
            last.then_inc(consts_made, 1)

            pool.wait_ge(wsm_hi, 1)
            pool.tensor_tensor(wsm[:, 1, WR], wsml[:, WR], wsm[:, 0, WR], ALU.subtract).then_inc(wsm_split, 1)
            for e in range(E):
                pool.wait_ge(w1_hi, e + 1)
                pool.tensor_tensor(w1[:, 1, e, :], w1s[:, e % W1_RING, :], w1[:, 0, e, :], ALU.subtract).then_inc(w1_split, 1)
            pool.memset(yT[:, :, :, SLOTS:], 0.0).then_inc(zeros_made, 1)
            pool.wait_ge(wsm_hi, 2)
            for w in range(2):
                o = WQ[w]
                pool.tensor_tensor(wsm[:, 1, o:o + 256].rearrange("p (f h) -> p f h", h=HEADS),
                                   wsml[:, o:o + 256].rearrange("p (h f) -> p f h", f=F),
                                   wsm[:, 0, o:o + 256].rearrange("p (f h) -> p f h", h=HEADS), ALU.subtract)
            pool.tensor_tensor(wsm[:, 1, WV:], wsml[:, WV:], wsm[:, 0, WV:], ALU.subtract).then_inc(wsm_split, 1)
            pool.wait_ge(wsm_split, 2)
            link(pool.memset(stack[4 * F:, :, :, :, :], 0.0))
            link(pool.memset(vst[:, :, :, :, :], 0.0))
            pool.memset(vst[:, :, :, :, 2 * HD:2 * HD + 1], 1.0)
            pool.memset(vst[:, :, :, :, VW + 2 * HD + 1:VW + 2 * HD + 2], 1.0).then_inc(zeros_made, 1)
            for s in ORDER:
                if s[0] == "sc":
                    n = nth[s]
                    pool.wait_ge(s_taken, n + 1)
                    d = amat[:, n % A_RING, :, 0:2 * P].rearrange("p h (c t) -> p h c t", t=P)
                    pool.affine_select(out=d, in_=d, pattern=[[0, 2], [0, 2], [1, P]], compare_op=ALU.is_ge,
                                       fill=0.0, base=0, channel_multiplier=-1).then_inc(a_ready, 1)

        @block.scalar
        def _(act):
            act.wait_ge(eps_made, 1)
            act.activation(warm[:, :], eps[:, :], ACT.Sqrt)

            def split_w1(e):
                act.wait_ge(w1_loaded[e], 16)
                act.activation(w1[:, 0, e, :], w1s[:, e % W1_RING, :], ACT.Copy).then_inc(w1_hi, 1)

            n_w1 = 0
            for s in ORDER:
                kind = s[0]
                n = nth[s]
                if kind == "ln1":
                    act.wait_ge(var_ready, n + 1)
                    act.activation(std[:, n % LN_RING, :], meanvar[:, n % LN_RING, :, 1], ACT.Sqrt,
                                   bias=eps[:, :]).then_inc(std_ready, 1)
                elif kind == "ex":
                    act.wait_ge(sel_ready, n + 1)
                    ld = ldiff[:, parity(*s[1:])]
                    act.activation(ld, ld, ACT.Exp).then_inc(exp_ready, 1)
                elif kind == "sq":
                    act.activation(warm[:, :], eps[:, :], ACT.Sqrt)
                elif by_scalar(s):
                    move_out(act, s)
                elif kind == "up":
                    _, l, g, e = s
                    if n >= 2:
                        act.wait_ge(y_ready, n - 1)
                    if n == 0:
                        wait_taken(act, ("bt",))
                    for c in range(HC):
                        if c % 2 == 0:
                            act.wait_ge(h_ready, 2 * n + c // 2 + 1)
                        ins = act.activation(hid[:, n % 2, c, :], psS[:, 2 * (n % 2) + c // 2, (c % 2) * GS:(c % 2 + 1) * GS],
                                             ACT.Relu, bias=biasT[:, e * HC + c:e * HC + c + 1])
                    ins.then_inc(h_taken, 1)
                elif kind == "down":
                    _, l, g, e = s
                    if n == 0:
                        act.wait_ge(zeros_made, 1)
                    act.wait_ge(y_ready, n + 1)
                    act.activation(yT[:, parity(l, g), :, e * CAP:(e + 1) * CAP],
                                   psY[:, n % 2, 0:GS].rearrange("p (b c) -> p b c", b=GB), ACT.Identity,
                                   bias=biasT[:, E * HC + e:E * HC + e + 1]).then_inc(y_taken, 1)
                elif kind == "yt":
                    _, l, g, k = s
                    wait_taken(act, s)
                    if k == 0 and n:
                        wait_ready(act, ("cb",) + units[units.index((l, g)) - 1] + (GB - 1,))
                    full, hi, _ = weighted_in(s)
                    act.activation(hi, full, ACT.Copy).then_inc(yh_ready, 1)
                elif kind == "qk":
                    _, p, w, c = s
                    wait_ready(act, s)
                    if p:
                        act.wait_ge(qk_stored[2 * w + c], 16 * p)
                    act.activation(qk16[:, w, c, 0, :], bank(s), ACT.Copy, scale=F ** -0.5 if w == 0 else 1.0)\
                        .then_inc(qk_hi, 1)
                elif kind == "sc":
                    act.wait_ge(s_ready, n + 1)
                    if n >= A_RING:
                        act.wait_ge(av_done, (n - A_RING) // 2 + 1)
                    act.activation(amat[:, n % A_RING, :, :], psS[:, 2 * (n % 2):2 * (n % 2) + 2, 0:T + P], ACT.Square)\
                        .then_inc(s_taken, 1)
                elif kind == "oT":
                    wait_ready(act, s)
                    act.activation(oT[:, :], bank(s)[:, 0:T], ACT.Copy).then_inc(taken(s), 1)
                if s == ("ln1", 0, 1):
                    act.wait_ge(wr_loaded, 16)
                    act.activation(wsm[:, 0, WR], wsml[:, WR], ACT.Copy).then_inc(wsm_hi, 1)
                for _ in range(SPLIT_BEHIND.get(s, 0)):
                    split_w1(n_w1)
                    n_w1 += 1
                if s == ("up", 0, 0, 1):
                    act.wait_ge(wqkv_loaded, 48)
                    for w in range(2):
                        o = WQ[w]
                        act.activation(wsm[:, 0, o:o + 256].rearrange("p (f h) -> p f h", h=HEADS),
                                       wsml[:, o:o + 256].rearrange("p (h f) -> p f h", f=F), ACT.Copy)
                    act.activation(wsm[:, 0, WV:], wsml[:, WV:], ACT.Copy).then_inc(wsm_hi, 1)
            assert n_w1 == E

        @block.vector
        def _(dve):
            steps = [0]

            def link(ins):
                steps[0] += 1
                ins.then_inc(dve_step, 1)
                dve.wait_ge(dve_step, steps[0])

            def over_experts(t):
                return t[:, :].unsqueeze(2).broadcast_to([P, GT, E])

            ranks = rank[:, :].unsqueeze(1).broadcast_to([P, GT, E])
            dve.wait_ge(consts_made, 1)
            for s in ORDER:
                kind = s[0]
                n = nth[s]
                if kind == "bt":
                    wait_ready(dve, s)
                    dve.tensor_copy(biasT[:, :], bank(s)[:, 0:E * HC + E]).then_inc(taken(s), 1)
                elif kind == "ln1":
                    _, which, p = s
                    if which == 0:
                        dve.wait_ge(x_loaded[p], 16)
                    else:
                        for b in (2 * p, 2 * p + 1):
                            wait_taken(dve, ("cb", 0, b // GB, b % GB) if which == 1 else ("wo", b))
                    for i in range(PTT):
                        ins = dve.bn_stats(stats[:, n % LN_RING, i, :], x[:, PTT * p + i, :])
                    link(ins)
                    for i in range(PTT):
                        ins = dve.bn_aggr(meanvar[:, n % LN_RING, i, :], stats[:, n % LN_RING, i, :])
                    ins.then_inc(var_ready, 1)
                elif kind == "lnx":
                    _, which, p = s
                    r = nth[("ln1",) + s[1:]] % LN_RING
                    dve.wait_ge(std_ready, nth[("ln1",) + s[1:]] + 1)
                    link(dve.reciprocal(rstd[:, r, :], std[:, r, :]))
                    for i in range(PTT):
                        ins = dve.tensor_scalar(xn[:, i, :], x[:, PTT * p + i, :], meanvar[:, r, i, 0:1],
                                                rstd[:, r, i:i + 1], ALU.subtract, ALU.mult)
                    link(ins)
                elif kind == "ln2":
                    _, which, p = s
                    parts = token_parts(which, p)[0]
                    if which == 1 and p:
                        wait_ready(dve, ("xt", 1, p - 1))
                    elif which == 2:
                        wait_ready(dve, ("dpl", 0, p // 2, GB - 1))
                    link(dve.tensor_copy(parts[:, 0], xn[:, :, :]))
                    dve.tensor_tensor(parts[:, 1], xn[:, :, :], parts[:, 0], ALU.subtract).then_inc(x_split, 1)
                elif kind == "xt":
                    dst = token_parts(*s[1:])[1]
                    wait_ready(dve, s)
                    dve.tensor_copy(dst.rearrange("p a t c -> p a (t c)"),
                                    bank16(s).rearrange("p (a n) -> p a n", a=2)).then_inc(taken(s), 1)
                elif kind == "lg":
                    _, l, g, half = s
                    wait_ready(dve, s)
                    dve.tensor_reduce(lg[:, PTT * half:PTT * (half + 1), :],
                                      bank(s)[:, 0:PTT * 2 * E].rearrange("p (t a e) -> p t e a", t=PTT, a=2),
                                      AX.X, ALU.add).then_inc(taken(s), 1)
                    if half:
                        wait_taken(dve, s)
                        link(dve.tensor_reduce(lmax[:, :], lg[:, :, :], AX.X, ALU.max))
                        dve.tensor_tensor(ldiff[:, parity(l, g)], lg[:, :, :], over_experts(lmax), ALU.subtract).then_inc(diff_ready, 1)
                elif kind == "c1":
                    ld = ldiff[:, parity(*s[1:])]
                    dve.wait_ge(diff_ready, n + 1)
                    link(dve.scalar_tensor_tensor(out=cand[:, :, :], in0=ld, scalar=0.0, in1=ranks,
                                                  op0=ALU.is_ge, op1=ALU.mult))
                    link(dve.tensor_reduce(cmax[:, :], cand[:, :, :], AX.X, ALU.max))
                    link(dve.tensor_tensor(sel1[:, :, :], cand[:, :, :], over_experts(cmax), ALU.is_equal))
                    link(dve.scalar_tensor_tensor(out=rest[:, :, :], in0=sel1[:, :, :], scalar=-BIG, in1=ld,
                                                  op0=ALU.mult, op1=ALU.add))
                elif kind == "c2":
                    link(dve.tensor_reduce(lmax[:, :], rest[:, :, :], AX.X, ALU.max))
                    link(dve.tensor_tensor(cand[:, :, :], rest[:, :, :], over_experts(lmax), ALU.is_ge))
                    link(dve.tensor_tensor(cand[:, :, :], cand[:, :, :], ranks, ALU.mult))
                    link(dve.tensor_reduce(cmax[:, :], cand[:, :, :], AX.X, ALU.max))
                    link(dve.tensor_tensor(rest[:, :, :], cand[:, :, :], over_experts(cmax), ALU.is_equal))
                    dve.tensor_tensor(sel[:, :, :, :].rearrange("p a b e -> p b a e"),
                                      sel1[:, :, :].rearrange("p (b a) e -> p b a e", a=TT),
                                      rest[:, :, :].rearrange("p (b a) e -> p b a e", a=TT), ALU.add).then_inc(sel_ready, 1)
                elif kind == "sm":
                    dve.wait_ge(exp_ready, n + 1)
                    lexp = ldiff[:, parity(*s[1:])]
                    link(dve.tensor_reduce(esum[:, :], lexp, AX.X, ALU.add))
                    link(dve.reciprocal(cmax[:, :], esum[:, :]))
                    link(dve.scalar_tensor_tensor(out=prob[:, :, :], in0=lexp, scalar=0.5,
                                                  in1=over_experts(cmax), op0=ALU.mult, op1=ALU.mult))
                    link(dve.tensor_copy(p16[:, :, 0, :], prob[:, :, :]))
                    dve.tensor_tensor(p16[:, :, 1, :], prob[:, :, :], p16[:, :, 0, :], ALU.subtract).then_inc(prob_split, 1)
                elif kind == "ps":
                    wait_ready(dve, s)
                    dve.scalar_tensor_tensor(out=key[:, :, :, :].rearrange("p a b e -> p (a b e)"),
                                             in0=bank(s)[:, 0:GT * E], scalar=1.0,
                                             in1=sel[:, :, :, :].rearrange("p a b e -> p (a b e)"),
                                             op0=ALU.add, op1=ALU.mult).then_inc(taken(s), 1)
                    wait_taken(dve, s)
                    if s[1]:
                        wait_ready(dve, ("ot", s[1] - 1, s[2], GB - 1))
                    for i in range(GB):
                        dve.tensor_tensor(
                            oh[:, parity(*s[1:]), TT * i:TT * i + TT, 0:SLOTS].rearrange("p a (e c) -> p a e c", e=E),
                            iota[:, :].unsqueeze(1).unsqueeze(1).broadcast_to([P, TT, E, CAP]),
                            key[:, :, i, :].unsqueeze(3).broadcast_to([P, TT, E, CAP]),
                            ALU.is_equal).then_inc(oh_ready, 1)
                elif kind == "pw":
                    _, l, g = s
                    if n == 0:
                        dve.wait_ge(consts_made, 2)
                    wait_ready(dve, s)
                    pm = yp[:, 0, 0:GB * KT * 2 * E]
                    if before(s, "yt"):
                        dve.wait_ge(yl_ready, before(s, "yt"))
                    dve.tensor_tensor(pm, bank(s)[:, 0:GB * KT * 2 * E], pmask[:, :], ALU.mult).then_inc(taken(s), 1)
                    wait_taken(dve, s)
                    link(dve.tensor_reduce(pslot[:, parity(l, g), :], pm.rearrange("p (s a) -> p s a", a=2 * E), AX.X, ALU.add))
                elif kind in ("ot", "dph", "dpl", "v", "xe"):
                    if not by_scalar(s):
                        move_out(dve, s)
                elif kind == "yt":
                    _, l, g, k = s
                    wait_ready(dve, s)
                    if n >= 2:
                        dve.wait_ge(yl_ready, n - 1)
                    k, rows = weighted(s)
                    nr = rows.stop - rows.start
                    dve.tensor_tensor(weighted_in(s)[0], bank(s)[:, 0:nr * P].rearrange("p (b c) -> p b c", c=C),
                                      pslot[:, parity(l, g), :].rearrange("p (b k) -> p b k", k=KT)[:, rows, k]
                                      .unsqueeze(2).broadcast_to([P, nr, C]), ALU.mult).then_inc(taken(s), 1)
                elif kind == "yl":
                    full, hi, lo = weighted_in(("yt",) + s[1:])
                    dve.wait_ge(yh_ready, n + 1)
                    dve.tensor_tensor(lo, full, hi, ALU.subtract).then_inc(yl_ready, 1)
                elif kind == "cb":
                    _, l, g, i = s
                    t = g * GT + TT * i
                    wait_ready(dve, s)
                    xt = x[:, t:t + TT, :].rearrange("p t c -> p (t c)")
                    dve.tensor_tensor(xt, bank(s)[:, 0:T], xt, ALU.add).then_inc(taken(s), 1)
                elif kind == "qk":
                    _, p, w, c = s
                    dve.wait_ge(qk_hi, n + 1)
                    dve.scalar_tensor_tensor(out=qk16[:, w, c, 1, :], in0=bank(s), scalar=F ** -0.5 if w == 0 else 1.0,
                                             in1=qk16[:, w, c, 0, :], op0=ALU.mult, op1=ALU.subtract).then_inc(taken(s), 1)
                elif kind == "ox":
                    wait_ready(dve, s)
                    r = bank(s).rearrange("p (g c) -> p g c", c=VW)
                    link(dve.tensor_scalar(den[:, :, :], r[:, :, 2 * HD:2 * HD + 2], DEN_EPS, None, ALU.add))
                    link(dve.reciprocal(rden[:, :, :], den[:, :, :]))
                    dve.tensor_tensor(onorm[:, :, :].rearrange("p t (g a d) -> p (t g) a d", a=2, d=HD),
                                      r[:, :, 0:2 * HD].rearrange("p g (a d) -> p g a d", a=2),
                                      rden[:, :, :].unsqueeze(3).broadcast_to([P, 16, 2, HD]), ALU.mult).then_inc(taken(s), 1)
                elif kind == "wo":
                    b = s[1]
                    wait_ready(dve, s)
                    xt = x[:, TT * b:TT * b + TT, :].rearrange("p t c -> p (t c)")
                    dve.tensor_tensor(xt, bank(s)[:, 0:T], xt, ALU.add).then_inc(taken(s), 1)

        @block.tensor
        def _(pe):
            mm = pe.matmul

            def take_bank(stage):
                k = item[stage]
                if k >= 2:
                    pe.wait_ge(bank_taken[k % 2], k // 2)

            def three(dst, lhs, rhs):
                mm(dst, lhs(0), rhs(0), start=True, stop=False)
                mm(dst, lhs(0), rhs(1), start=False, stop=False)
                return mm(dst, lhs(1), rhs(0), start=False, stop=True)

            def combine_tiles(dst, l, g, i, tiles, opened=False):
                for t in range(TT):
                    for k in tiles:
                        for a in range(2):
                            ins = mm(dst[:, t * P:(t + 1) * P], ohT[:, parity(l, g), i, k, t * P:(t + 1) * P],
                                     y16[:, a, i, k * P:(k + 1) * P], start=(not opened and k + a == 0),
                                     stop=(k == KT - 1 and a == 1 and (t == TT - 1 or not opened)))
                return ins

            pe.wait_ge(ones_made, 1)
            def keep_warm(count):
                for _ in range(count):
                    mm(psS[:, 0, 0:P], ones16[:, :], ones16[:, :], start=True, stop=True)

            keep_warm(WARM_UP)
            pe.wait_ge(consts_made, 1)
            for s in ORDER:
                kind = s[0]
                n = nth[s]
                if kind in MISC:
                    if not last_unit(s):
                        take_bank(s)
                    m = bank(s)
                last = None
                if kind == "warm":
                    keep_warm(s[1])
                elif kind == "bt":
                    pe.wait_ge(bias_loaded, 32)
                    nb = E * HC + E
                    last = pe.transpose(m[:, 0:nb], bias_rows, ident[0:nb, 0:nb])
                elif kind == "xt":
                    pe.wait_ge(x_split, nth[("ln2",) + s[1:]] + 1)
                    src = token_parts(*s[1:])[0]
                    m16 = bank16(s)
                    for a in range(2):
                        for t in range(PTT):
                            o = (PTT * a + t) * P
                            last = pe.transpose(m16[:, o:o + P], src[:, a, t, :], ident16[:, :])
                elif kind == "lg":
                    _, l, g, half = s
                    wait_taken(pe, ("xt", 2 * l, 2 * g + half))
                    if n == 0:
                        pe.wait_ge(wsm_split, 1)
                    for t in range(PTT):
                        for a in range(2):
                            last = mm(m[:, t * 2 * E:(t + 1) * 2 * E], xTf[:, a, PTT * half + t, :], wsm[:, :, WR],
                                      start=(a == 0), stop=(a == 1))
                elif kind == "ps":
                    pe.wait_ge(sel_ready, n + 1)
                    w = GB * E
                    mm(m[:, 0:w], upper16[:, :], sel[:, 0, :, :], start=True, stop=True)
                    mm(m[:, w:2 * w], ones16[:, :], sel[:, 0, :, :], start=True, stop=False)
                    last = mm(m[:, w:2 * w], upper16[:, :], sel[:, 1, :, :], start=False, stop=True)
                elif kind == "ot":
                    i = s[3]
                    m16 = bank16(s)
                    for k in range(KT):
                        for t in range(TT):
                            o = (k * TT + t) * P
                            last = pe.transpose(m16[:, o:o + P], oh[:, parity(*s[1:3]), TT * i + t, k * P:(k + 1) * P], ident16[:, :])
                elif kind == "pw":
                    pe.wait_ge(prob_split, n + 1)
                    if n == 0:
                        pe.wait_ge(consts_made, 2)
                    for i in range(GB):
                        for k in range(KT):
                            o = (i * KT + k) * 2 * E
                            for t in range(TT):
                                last = mm(m[:, o:o + 2 * E], oh[:, parity(*s[1:]), TT * i + t, k * P:(k + 1) * P],
                                          p16[:, TT * i + t, :, :], start=(t == 0), stop=(t == TT - 1))
                elif kind in ("dph", "dpl"):
                    i = s[3]
                    if kind == "dph":
                        pe.wait_ge(oh_ready, nth[("ps",) + s[1:3]] * GB + i + 1)
                    for t in range(TT):
                        last = mm(m[:, 0:SLOTS], xf[:, parity(*s[1:3]), int(kind == "dpl"), TT * i + t, :],
                                  oh[:, parity(*s[1:3]), TT * i + t, 0:SLOTS],
                                  start=(t == 0), stop=(t == TT - 1))
                elif kind == "up":
                    _, l, g, e = s
                    u = parity(l, g)
                    if e == 0:
                        for i in range(GB):
                            wait_taken(pe, ("dph", l, g, i))
                            wait_taken(pe, ("dpl", l, g, i))
                    if n < E:
                        pe.wait_ge(w1_split, e + 1)
                    if n >= 2:
                        pe.wait_ge(h_taken, n - 1)
                    if before(s, "sc"):
                        pe.wait_ge(s_taken, before(s, "sc"))
                    for c in range(HC):
                        dst = psS[:, 2 * (n % 2) + c // 2, (c % 2) * GS:(c % 2 + 1) * GS]
                        ins = three(dst, lambda a: w1[:, a, e, c * P:(c + 1) * P], lambda a: xe[:, u, a, e, :])
                        if c % 2:
                            ins.then_inc(h_ready, 1)
                elif kind == "down":
                    _, l, g, e = s
                    pe.wait_ge(h_taken, n + 1)
                    if n < E:
                        pe.wait_ge(w2_loaded[e], 16)
                    if n >= 2:
                        pe.wait_ge(y_taken, n - 1)
                    if before(s, "xe"):
                        pe.wait_ge(xy_taken, before(s, "xe"))
                    for c in range(HC):
                        ins = mm(psY[:, n % 2, 0:GS], w2[:, e, c, :], hid[:, n % 2, c, :], start=(c == 0), stop=(c == HC - 1))
                    ins.then_inc(y_ready, 1)
                elif kind == "yt":
                    _, l, g, k = s
                    pe.wait_ge(y_taken, nth[("down", l, g, min(((k + 1) * P - 1) // CAP, E - 1))] + 1)
                    if n == 0:
                        pe.wait_ge(zeros_made, 1)
                    k, rows = weighted(s)
                    for j, i in enumerate(range(rows.start, rows.stop)):
                        last = pe.transpose(m[:, j * P:(j + 1) * P], yT[:, parity(l, g), i, k * P:(k + 1) * P], ident[:, :])
                elif kind == "ca":
                    pe.wait_ge(yl_ready, nth[("yl",) + s[1:3] + (1,)] + 1)
                    pe.wait_ge(h_taken, before(s, "up"))
                    u = parity(*s[1:3])
                    for i in range(GB):
                        wait_taken(pe, ("ot",) + s[1:3] + (i,))
                        mm(psS[:, i, 0:T], ones16[:, :], oh[:, u, 0:T // (SP_ - SLOTS), SLOTS:], start=True, stop=False)
                        combine_tiles(psS[:, i, :], *s[1:3], i, (0, 1), opened=True)
                elif kind == "cb":
                    _, l, g, i = s
                    k = KT - 1 + (2 * i // GB if last_unit(s) else 0)
                    pe.wait_ge(yl_ready, nth[("yl", l, g, k)] + 1)
                    wait_taken(pe, ("ot", l, g, i))
                    if last_unit(s):
                        last = combine_tiles(m, l, g, i, (2,), opened=True)
                    else:
                        last = combine_tiles(m, l, g, i, (0, 1, 2))
                elif kind == "qk":
                    _, p, w, c = s
                    wait_taken(pe, ("xt", 1, p))
                    if n == 0:
                        pe.wait_ge(wsm_split, 2)
                    o = WQ[w] + c * P
                    last = three(m, lambda a: wsm[:, a, o:o + P],
                                 lambda a: xTa[:, a, :, :].rearrange("p t c -> p (t c)"))
                elif kind == "v":
                    wait_taken(pe, ("xt", 1, s[1] // 2))
                    for t in range(TT):
                        last = three(m[:, t * P:(t + 1) * P], lambda a: xTa[:, a, TT * (s[1] % 2) + t, :], lambda a: wsm[:, a, WV:WV + C])
                elif kind == "sc":
                    _, b, pair = s
                    if pair == 0:
                        pe.wait_ge(stack_loaded[b % 2], 5 * 16 * (b // 2 + 1))
                        if b == 0:
                            pe.wait_ge(zeros_made, 2)
                    if n >= 2:
                        pe.wait_ge(s_taken, n - 1)
                    else:
                        pe.wait_ge(h_taken, before(s, "up"))
                    for j in range(2):
                        h = HEAD_ORDER[2 * pair + j]
                        d = psS[:, 2 * (n % 2) + j, :]
                        q, k = stack[:, b % 2, 0, h, :], stack[:, b % 2, 1, h, :]
                        mm(d[:, P:P + T], k[:, 0:P], q, start=True, stop=True)
                        ins = mm(d[:, 0:P], k[:, P:T], q[:, P:T], start=True, stop=True)
                    ins.then_inc(s_ready, 1)
                elif kind == "av":
                    _, b, q = s
                    half = q // 2
                    if q == 0:
                        wait_taken(pe, ("v", b))
                    pe.wait_ge(a_ready, 2 * n + 2)
                    if q % 2 == 0:
                        if b:
                            pe.wait_ge(xy_taken, 2 * (b - 1) + half + 1)
                        else:
                            pe.wait_ge(y_taken, before(s, "down"))
                    for st in range(TT):
                        for j in range(4):
                            h = HEAD_ORDER[4 * q + j]
                            col = VW * ((h % 8) // 2)
                            a = amat[:, (2 * n + j // 2) % A_RING, j % 2, :]
                            v = vst[:, b % 4, st, h // 2, VW * (h % 2):VW * (h % 2) + VW]
                            if st == 0:
                                mm(psY[col:col + VW, half, 0:T], v, a[:, P:P + T], start=(q % 2 == 0), stop=False)
                            else:
                                ins = mm(psY[col:col + VW, half, P:T], v, a[:, 0:P], start=False, stop=(q % 2 == 1))
                    ins.then_inc(av_done, 1)
                elif kind == "ox":
                    b = s[1]
                    pe.wait_ge(xy_taken, 2 * b + 2)
                    for t in range(TT):
                        for half in range(2):
                            o = (2 * t + half) * P
                            last = pe.transpose(m[:, o:o + P], xy[:, b % 2, half, t * P:(t + 1) * P], ident[:, :])
                elif kind == "oT":
                    wait_taken(pe, ("ox", s[1]))
                    for t in range(TT):
                        last = pe.transpose(m[:, t * P:(t + 1) * P], onorm[:, t, :], ident[:, :])
                elif kind == "wo":
                    wait_taken(pe, ("oT", s[1]))
                    if n == 0:
                        pe.wait_ge(wo_loaded, 16)
                    for t in range(TT):
                        last = mm(m[:, t * P:(t + 1) * P], oT[:, t * P:(t + 1) * P], wo[:, :], start=True, stop=True)
                if kind in MISC:
                    last.then_inc(bank_ready[item[s] % 2], 1)


INPUTS = ["L0_attn_hidden_states", "L0_attn_Wq", "L0_attn_Wk", "L0_attn_Wv", "L0_attn_Wo",
          "L0_ffn_Wr", "L0_ffn_W1", "L0_ffn_b1", "L0_ffn_W2", "L0_ffn_b2"]


def kernel(**inputs):
    import numpy as np
    import concourse.bacc as bacc
    from concourse.bass_utils import run_bass_kernel_spmd

    nc = bacc.Bacc("TRN2", target_bir_lowering=False, num_devices=1)
    arrays, args = {}, []
    for name in INPUTS:
        a = np.ascontiguousarray(inputs[name])
        arrays[f"in_{name}"] = a
        args.append(nc.dram_tensor(f"in_{name}", a.shape, mybir.dt.from_np(a.dtype), kind="ExternalInput").ap())
    args.append(nc.dram_tensor("out", (B, T, C), mybir.dt.float32, kind="ExternalOutput").ap())
    macaron_program(nc, *args)
    return run_bass_kernel_spmd(nc, [arrays], core_ids=[0]).results[0]["out"]
```
